# Optimizing a Trainium2 kernel written in Bass

```python
import numpy as np
import jax
import jax.numpy as jnp

def _softmax(x, axis=-1):
    return jax.nn.softmax(x, axis=axis)

def _gelu(x):
    return jax.nn.gelu(x, approximate=True)

def _silu(x):
    return jax.nn.silu(x)

def _sigmoid(x):
    return jax.nn.sigmoid(x)

def _layernorm(x, axis=-1, eps=1e-05):
    m = jnp.mean(x, axis=axis, keepdims=True)
    v = jnp.var(x, axis=axis, keepdims=True)
    return (x - m) / jnp.sqrt(v + eps)

def _scatter_add(tgt, idx, src, axis=0):
    return tgt.at[idx].add(src)

def _segment_sum(src, seg, n):
    return jax.ops.segment_sum(src, seg, n)
kernel_name = 'mk_prb_d1_jaxref_r8_05ca56'

def setup_inputs(seed: int=0):
    np.random.seed(seed)
    _w = jnp.asarray

    def _L0_attn_setup():
        import jax, jax.numpy as jnp
        import numpy as np
        EPS = 1e-06

        def _causal_depthwise_conv(x, conv_w, conv_b):
            B, L, d = x.shape
            lhs = jnp.transpose(x, (0, 2, 1))
            out = jax.lax.conv_general_dilated(lhs, conv_w, window_strides=(1,), padding=[(3, 0)], feature_group_count=d, dimension_numbers=('NCH', 'OIH', 'NCH'))
            out = out + conv_b[None, :, None]
            return jnp.transpose(out, (0, 2, 1))
        key = jax.random.key(seed)
        ks = jax.random.split(key, 8)
        B, L, d = (4, 512, 128)
        x = jax.random.normal(ks[0], (B, L, d), dtype=jnp.float32)
        conv_w = jax.random.normal(ks[1], (d, 1, 4), dtype=jnp.float32) * 0.02
        conv_b = jnp.zeros((d,), dtype=jnp.float32)
        lim = 1.0 / np.sqrt(d)
        W_r = jax.random.uniform(ks[2], (d, d), jnp.float32, -lim, lim)
        b_r = jax.random.uniform(ks[3], (d,), jnp.float32, -lim, lim)
        W_i = jax.random.uniform(ks[4], (d, d), jnp.float32, -lim, lim)
        b_i = jax.random.uniform(ks[5], (d,), jnp.float32, -lim, lim)
        log_a = jnp.full((d,), 7.5, dtype=jnp.float32)
        W_out = jax.random.uniform(ks[6], (d, d), jnp.float32, -lim, lim)
        gamma = jnp.ones((d,), dtype=jnp.float32)
        return {'x': x, 'conv_w': conv_w, 'conv_b': conv_b, 'W_r': W_r, 'b_r': b_r, 'W_i': W_i, 'b_i': b_i, 'log_a': log_a, 'W_out': W_out, 'gamma': gamma}
    _L0_attn_in = _L0_attn_setup()

    def _L0_ffn_setup():
        import math
        import jax, jax.numpy as jnp
        import numpy as np
        B, S, D, F, E = (8, 256, 128, 512, 8)
        CAPACITY_FACTOR = 1.0
        key = jax.random.key(seed)
        k1, k2, k3, k4 = jax.random.split(key, 4)
        x = jax.random.normal(k1, (B, S, D), dtype=jnp.float32)
        Wr = jax.random.normal(k2, (D, E), dtype=jnp.float32) * (1.0 / math.sqrt(D))
        W1 = jax.random.normal(k3, (E, D, F), dtype=jnp.float32) * (1.0 / math.sqrt(D))
        W2 = jax.random.normal(k4, (E, F, D), dtype=jnp.float32) * (1.0 / math.sqrt(F))
        return {'x': x, 'Wr': Wr, 'W1': W1, 'W2': W2}
    _L0_ffn_in = _L0_ffn_setup()
    _d = {'L0_attn_x': _L0_attn_in['x'], 'L0_attn_conv_w': _L0_attn_in['conv_w'], 'L0_attn_conv_b': _L0_attn_in['conv_b'], 'L0_attn_W_r': _L0_attn_in['W_r'], 'L0_attn_b_r': _L0_attn_in['b_r'], 'L0_attn_W_i': _L0_attn_in['W_i'], 'L0_attn_b_i': _L0_attn_in['b_i'], 'L0_attn_log_a': _L0_attn_in['log_a'], 'L0_attn_W_out': _L0_attn_in['W_out'], 'L0_attn_gamma': _L0_attn_in['gamma'], 'L0_ffn_Wr': _L0_ffn_in['Wr'], 'L0_ffn_W1': _L0_ffn_in['W1'], 'L0_ffn_W2': _L0_ffn_in['W2']}
    _x0 = _d['L0_attn_x']
    _d['L0_attn_x'] = jax.random.normal(jax.random.fold_in(jax.random.key(seed), 1), (16, 256, 128), dtype=_x0.dtype)
    del _x0
    return _d

def reference(L0_attn_x, L0_attn_conv_w, L0_attn_conv_b, L0_attn_W_r, L0_attn_b_r, L0_attn_W_i, L0_attn_b_i, L0_attn_log_a, L0_attn_W_out, L0_attn_gamma, L0_ffn_Wr, L0_ffn_W1, L0_ffn_W2):

    def _L0_attn_ref(x, conv_w, conv_b, W_r, b_r, W_i, b_i, log_a, W_out, gamma):
        import jax, jax.numpy as jnp
        import numpy as np
        EPS = 1e-06

        def _causal_depthwise_conv(x, conv_w, conv_b):
            B, L, d = x.shape
            lhs = jnp.transpose(x, (0, 2, 1))
            out = jax.lax.conv_general_dilated(lhs, conv_w, window_strides=(1,), padding=[(3, 0)], feature_group_count=d, dimension_numbers=('NCH', 'OIH', 'NCH'))
            out = out + conv_b[None, :, None]
            return jnp.transpose(out, (0, 2, 1))
        B, L, d = x.shape
        x_conv = _causal_depthwise_conv(x, conv_w, conv_b)
        r_t = jax.nn.sigmoid(x_conv @ W_r.T + b_r)
        i_t = jax.nn.sigmoid(x_conv @ W_i.T + b_i)
        a_base = jax.nn.sigmoid(log_a)
        a_t = a_base[None, None, :] ** (8.0 * r_t)
        inp = i_t * x_conv
        scale = jnp.sqrt(jnp.clip(1.0 - a_t * a_t, 0.0))

        def step(h, ab):
            a, b = ab
            h = a * h + b
            return (h, h)
        xs = (jnp.moveaxis(a_t, 1, 0), jnp.moveaxis(scale * inp, 1, 0))
        h0 = jnp.zeros((B, d), dtype=x.dtype)
        _, hs = jax.lax.scan(step, h0, xs)
        out = jnp.moveaxis(hs, 0, 1)
        out = out @ W_out.T
        rms = jax.lax.rsqrt(jnp.mean(out * out, axis=-1, keepdims=True) + EPS)
        return out * rms * gamma

    def _L0_ffn_ref(x, Wr, W1, W2):
        import math
        import jax, jax.numpy as jnp
        import numpy as np
        B, S, D, F, E = (8, 256, 128, 512, 8)
        CAPACITY_FACTOR = 1.0
        b, s, d = x.shape
        t = b * s
        cap = max(math.ceil(t * CAPACITY_FACTOR / E), 1)
        xf = x.reshape(t, d)
        probs = jax.nn.softmax(xf.astype(jnp.float32) @ Wr, axis=-1)
        eidx = jnp.argmax(probs, axis=-1)
        p_tok = jnp.take_along_axis(probs, eidx[:, None], axis=1)[:, 0]
        onehot = jax.nn.one_hot(eidx, E, dtype=jnp.int32)
        rank_all = jnp.cumsum(onehot, axis=0) - onehot
        rank = jnp.take_along_axis(rank_all, eidx[:, None], axis=1)[:, 0]
        keep = rank < cap
        slot = jnp.where(keep, rank, cap)
        dispatch = jnp.zeros((E, cap + 1), dtype=jnp.int32).at[eidx, slot].set(jnp.arange(t, dtype=jnp.int32))
        valid = jnp.zeros((E, cap + 1), dtype=bool).at[eidx, slot].set(keep)
        dispatch = dispatch[:, :cap]
        valid = valid[:, :cap]
        xe = xf[dispatch]
        h = jnp.maximum(jnp.einsum('ecd,edf->ecf', xe, W1), 0.0)
        ye = jnp.einsum('ecf,efd->ecd', h, W2)
        pe = p_tok[dispatch]
        ye = ye * (pe * valid.astype(ye.dtype))[:, :, None]
        y = jnp.zeros((t, d), dtype=x.dtype).at[dispatch.reshape(-1)].add(ye.reshape(E * cap, d).astype(x.dtype))
        return y.reshape(b, s, d)
    x = L0_attn_x
    xn = _layernorm(x, axis=-1)
    x = x + _L0_attn_ref(xn, L0_attn_conv_w, L0_attn_conv_b, L0_attn_W_r, L0_attn_b_r, L0_attn_W_i, L0_attn_b_i, L0_attn_log_a, L0_attn_W_out, L0_attn_gamma) + _L0_ffn_ref(xn, L0_ffn_Wr, L0_ffn_W1, L0_ffn_W2)
    return x

_drawn_inputs = setup_inputs


def setup_inputs(seed=0):
    import zlib

    import numpy as np

    out = dict(_drawn_inputs(seed))
    spreads = {'L0_attn_conv_b': (0.0, 0.1), 'L0_attn_log_a': (7.5, 0.2), 'L0_attn_gamma': (1.0, 0.2)}
    factors = {'L0_attn_W_r': 6.597, 'L0_attn_b_r': 8.0, 'L0_attn_b_i': 2.676}
    for name, (base, spread) in spreads.items():
        noise = np.random.default_rng([zlib.crc32(name.encode()), seed]).standard_normal(out[name].shape)
        drawn = base * np.exp(spread * noise) if base else spread * noise
        out[name] = jnp.asarray(drawn.astype(out[name].dtype))
    for name, factor in factors.items():
        out[name] = (out[name] * factor).astype(out[name].dtype)
    return out
```

```python
from contextlib import ExitStack

import concourse.bass as bass
from concourse import mybir

F32 = mybir.dt.float32
I32 = mybir.dt.int32
ALU = mybir.AluOpType
ACT = mybir.ActivationFunctionType
AX_X = mybir.AxisListType.X

P = 128
B, L, D = 16, 256, 128
T = B * L
E, F = 8, 512
CAP = T // E
C = 4
J = T // C // P
NT = C * J
TC = T // C
SC = TC // L
HC = TC // 2
KF = F // P
ST = CAP // P
NS = E * ST
TAPS = 4
LN_EPS = 1e-5
RMS_EPS = 1e-6
LOGA_FLOOR = -20.0

WR_T, WI_T, WO_T = 0, D, 2 * D
ROUTER = 3 * D
CONV_W = ROUTER + E
CONV_B, BIAS_R, BIAS_I, LOG_A = (CONV_W + TAPS + i for i in range(4))
NPAR = LOG_A + 1


def rglru_moe_kernel(nc, x, params, gamma, w1, w2, xn_rows, out):
    x_rows = x.rearrange("b l d -> (b l) d")
    out_rows = out.rearrange("b l d -> (b l) d")

    def chunk_rows(dram, c):
        return dram[c * TC:(c + 1) * TC, :].rearrange("(p j) d -> p (j d)", p=P)

    with ExitStack() as ctx:
        def sb(name, shape, dt=F32):
            return ctx.enter_context(nc.sbuf_tensor(name, shape, dt))

        def psum(name):
            return ctx.enter_context(nc.psum_tensor(name, [P, 512], F32))

        def sem(name):
            return ctx.enter_context(nc.semaphore(name))

        par = sb("par", [P, NPAR])
        gam = sb("gam", [P, D])
        w1_sb = sb("w1_sb", [P, E * F])
        w2_sb = sb("w2_sb", [P, E * KF * D])
        x_tok = sb("x_tok", [P, NT * D])
        xn_tok = sb("xn_tok", [P, NT * D])
        xnT = sb("xnT", [P, T])
        xc = sb("xc", [P, T])
        dec = sb("dec", [P, T])
        inp = sb("inp", [P, T])
        sca = sb("sca", [P, T])
        h_sb = sb("h_sb", [P, 2, KF * CAP])
        xgT = sb("xgT", [P, 2, CAP])
        ident = sb("ident", [P, P])
        upper = sb("upper", [P, P])
        ones = sb("ones", [P, P])
        iota_low = sb("iota_low", [P, P])
        tok_id = sb("tok_id", [P, NT])
        desc = sb("desc", [P, NT, E])
        e_base = sb("e_base", [P, C, E, J])
        jmask = sb("jmask", [P, C, E, J])
        eps = sb("eps", [P, 3])
        quarter = eps[:, 2:3]
        stats = sb("stats", [P, NT, 6])
        mv = sb("mv", [P, NT, 2])
        std = sb("std", [P, NT])
        rstd = sb("rstd", [P, NT])
        half_b = sb("half_b", [P, 2])
        lna = sb("lna", [P, 8])
        top = sb("top", [P, NT])
        eq = sb("eq", [P, NT, E])
        best = sb("best", [P, NT])
        onehot = sb("onehot", [P, C, E, J])
        count = sb("count", [P, C, E, J])
        wide = sb("wide", [P, C, E, J])
        picked = sb("picked", [P, C, J, E])
        shifted = sb("shifted", [P, NT, E])
        psumx = sb("psumx", [P, NT])
        prob = sb("prob", [P, NT])
        slot = sb("slot", [P, NT])
        rank = sb("rank", [P, NT])
        keep = sb("keep", [P, NT])
        small = sb("small", [P, 8, E])
        over = sb("over", [P, NT])
        dslot = sb("dslot", [P, NT])
        slot_i = sb("slot_i", [P, NT], I32)
        hi_i = sb("hi_i", [P, NT], I32)
        lo_i = sb("lo_i", [P, NT], I32)
        lo_f = sb("lo_f", [P, NT])
        hi_eq = sb("hi_eq", [P, NT, NS])
        hi_val = sb("hi_val", [P, NT, 2, NS])
        idx = sb("idx", [P, NS], I32)
        p_slot = sb("p_slot", [P, NS])
        sq = sb("sq", [P, D])
        ssq = sb("ssq", [P, NT])
        rms = sb("rms", [P, NT])
        low_eq = sca
        hs = xnT
        gathered = x_tok
        attn = xn_tok

        tp = [psum("tp0"), psum("tp1")]
        gate = [psum("gate0"), psum("gate1")]
        hid = [psum("hid0"), psum("hid1")]
        yb = psum("yb")
        rt = psum("rt")
        logits = rt[:, 0:NT * E]
        before = rt[:, 256:256 + C * E]
        totals = rt[:, 320:320 + E]
        table = yb[:, 0:2 * NS]
        obank = [gate[0], gate[1], rt]

        x_in = [sem(f"x_in{c}") for c in range(C)]
        par_in = sem("par_in")
        gam_in = sem("gam_in")
        w1_in = sem("w1_in")
        w2_in = sem("w2_in")
        x_out = sem("x_out")
        xn_out = sem("xn_out")
        consts = sem("consts")
        fill = sem("fill")
        stat_done = sem("stat_done")
        aggr_done = sem("aggr_done")
        std_done = sem("std_done")
        rstd_done = sem("rstd_done")
        norm_done = sem("norm_done")
        tp_done = sem("tp_done")
        xnT_done = sem("xnT_done")
        logits_done = sem("logits_done")
        route = sem("route")
        counted = sem("counted")
        offsets = sem("offsets")
        shift_done = sem("shift_done")
        exp_done = sem("exp_done")
        hi_done = sem("hi_done")
        low_done = sem("low_done")
        table_done = sem("table_done")
        idx_done = sem("idx_done")
        coef = sem("coef")
        lna_act = sem("lna_act")
        conv_done = sem("conv_done")
        conv_tap = sem("conv_tap")
        gate_mm = sem("gate_mm")
        gate_free = sem("gate_free")
        tanh_r = sem("tanh_r")
        tanh_i = sem("tanh_i")
        decay_done = sem("decay_done")
        square_done = sem("square_done")
        clip_done = sem("clip_done")
        scale_done = sem("scale_done")
        gated_done = sem("gated_done")
        input_done = sem("input_done")
        scan_done = sem("scan_done")
        o_mm = sem("o_mm")
        ssq_done = sem("ssq_done")
        rms_std = sem("rms_std")
        rms_done = sem("rms_done")
        attn_done = sem("attn_done")
        gather_in = [sem(f"gather_in{e}") for e in range(E)]
        xg_tp = sem("xg_tp")
        xg_done = sem("xg_done")
        h_mm = sem("h_mm")
        h_done = sem("h_done")
        y_mm = sem("y_mm")
        y_done = sem("y_done")
        scattered = sem("scattered")
        attn_out = sem("attn_out")

        block = ctx.enter_context(nc.Block())

        BEFORE_ATTN = 4

        @block.sync
        def _(sp):
            for c in range(C):
                sp.dma_start(x_tok[:, c * J * D:(c + 1) * J * D], chunk_rows(x_rows, c)).then_inc(x_in[c], 16)
                if c == 0:
                    sp.dma_start(par[:, :], params).then_inc(par_in, 16)
            sp.dma_start(gam[:, :], gamma.partition_broadcast(P)).then_inc(gam_in, 16)
            for c in range(C):
                sp.wait_ge(x_in[c], 16)
                sp.dma_start(chunk_rows(out_rows, c), x_tok[:, c * J * D:(c + 1) * J * D]).then_inc(x_out, 16)
            for c in range(C):
                sp.wait_ge(norm_done, J * (c + 1))
                sp.dma_start(chunk_rows(xn_rows, c), xn_tok[:, c * J * D:(c + 1) * J * D]).then_inc(xn_out, 16)
            sp.dma_start(w1_sb[:, :], w1).then_inc(w1_in, 16)
            sp.dma_start(w2_sb[:, :], w2).then_inc(w2_in, 16)

        @block.gpsimd
        def _(pool):
            g = nc.gpsimd
            g.memset(eps[:, 0:1], LN_EPS).then_inc(consts, 1)
            g.memset(eps[:, 1:2], RMS_EPS).then_inc(consts, 1)
            g.memset(eps[:, 2:3], 0.25).then_inc(consts, 1)
            g.memset(ident[:, :], 0.0).then_inc(fill, 1)
            g.memset(ones[:, :], 1.0).then_inc(fill, 1)
            pool.wait_ge(fill, 2)
            g.affine_select(out=ident[:, :], in_=ident[:, :], compare_op=ALU.not_equal, fill=1.0, base=0,
                            pattern=[[-1, P]], channel_multiplier=1).then_inc(consts, 1)
            g.affine_select(out=upper[:, :], in_=ones[:, :], compare_op=ALU.is_gt, fill=0.0, base=0,
                            pattern=[[1, P]], channel_multiplier=-1).then_inc(consts, 1)
            exact = dict(allow_small_or_imprecise_dtypes=True)
            g.iota(desc[:, :, :], [[0, NT], [-1, E]], base=E, channel_multiplier=0, **exact).then_inc(consts, 1)
            g.memset(jmask[:, :, :, :], 1.0).then_inc(fill, 1)
            pool.wait_ge(fill, 3)
            g.memset(jmask[:, :, :, 0:1], 0.0).then_inc(consts, 1)
            g.iota(e_base[:, :, :, :], [[0, C], [CAP, E], [0, J]], base=-1, channel_multiplier=0,
                   **exact).then_inc(consts, 1)
            g.iota(iota_low[:, :], [[1, P]], base=0, channel_multiplier=0, **exact).then_inc(consts, 1)
            g.iota(tok_id[:, :], [[TC, C], [1, J]], base=0, channel_multiplier=J, **exact).then_inc(consts, 1)

            def gather(e):
                for s in range(e * ST, (e + 1) * ST):
                    g.indirect_dma_start(gathered[:, s * D:(s + 1) * D], None, xn_rows,
                                         bass.IndirectOffsetOnAxis(ap=idx[:, s:s + 1], axis=0)
                                         ).then_inc(gather_in[e], 16)

            def scatter(e):
                pool.wait_ge(y_done, e + 1)
                for s in range(e * ST, (e + 1) * ST):
                    g.indirect_dma_start(out_rows, bass.IndirectOffsetOnAxis(ap=idx[:, s:s + 1], axis=0),
                                         gathered[:, s * D:(s + 1) * D], None,
                                         compute_op=ALU.add).then_inc(scattered, 16)

            pool.wait_ge(xn_out, 16 * C)
            pool.wait_ge(x_out, 16 * C)
            pool.wait_ge(idx_done, 1)
            for e in range(4):
                gather(e)
            for e in range(4, E):
                scatter(e - 4)
                gather(e)
            pool.wait_ge(scattered, 16 * ST * BEFORE_ATTN)
            for c in range(C):
                pool.wait_ge(attn_done, J * (c + 1))
                g.dma_start(chunk_rows(out_rows, c), attn[:, c * J * D:(c + 1) * J * D],
                            accum_op=ALU.add).then_inc(attn_out, 16)
            pool.wait_ge(attn_out, 16 * C)
            for e in range(BEFORE_ATTN, E):
                scatter(e)
            pool.wait_ge(scattered, 16 * NS)

        @block.tensor
        def _(pe):
            mm = nc.tensor.matmul
            pe.wait_ge(consts, 5)

            for n in range(2 * C):
                c = n // 2
                pe.wait_ge(norm_done, 4 * (n + 1))
                if n >= 2:
                    pe.wait_ge(xnT_done, n - 1)
                for i in range(4):
                    t = 4 * n + i
                    last = nc.tensor.transpose(tp[n % 2][:, i * P:(i + 1) * P],
                                               xn_tok[:, t * D:(t + 1) * D], ident[:, :])
                last.then_inc(tp_done, 1)
                if n == 0:
                    pe.wait_ge(par_in, 16)
                if n >= 1:
                    pe.wait_ge(xnT_done, n)
                    for t in range(4 * (n - 1), 4 * n):
                        cc, j = t // J, t % J
                        last = mm(logits[:, t * E:(t + 1) * E], xnT[:, cc * TC + j:(cc + 1) * TC:J],
                                  par[:, ROUTER:ROUTER + E], start=True, stop=True)
            pe.wait_ge(xnT_done, 2 * C)
            for t in range(NT - 4, NT):
                cc, j = t // J, t % J
                last = mm(logits[:, t * E:(t + 1) * E], xnT[:, cc * TC + j:(cc + 1) * TC:J],
                          par[:, ROUTER:ROUTER + E], start=True, stop=True)
            last.then_inc(logits_done, 1)

            pe.wait_ge(consts, 10)
            pe.wait_ge(counted, 1)
            rows = count[:, :, :, J - 1]
            mm(before, upper[:, :], rows, start=True, stop=False)
            for s in range(1, C):
                mm(before[:, s * E:], ones[:, :], rows[:, 0:C - s, :], start=False, stop=(s == C - 1))
            for c in range(C):
                last = mm(totals, ones[:, :], rows[:, c, :], start=(c == 0), stop=(c == C - 1))
            last.then_inc(offsets, 1)

            pe.wait_ge(hi_done, 2)
            for t in range(NT):
                pe.wait_ge(low_done, t + 1)
                last = mm(table, low_eq[:, t * P:(t + 1) * P], hi_val[:, t, :, :],
                          start=(t == 0), stop=(t == NT - 1))
            last.then_inc(table_done, 1)

            def gates(c):
                pe.wait_ge(conv_done, c + 1)
                for i, w in enumerate((WR_T, WR_T, WI_T, WI_T)):
                    n = 4 * c + i
                    if n >= 2:
                        pe.wait_ge(gate_free, n - 1)
                    mm(gate[n % 2][:, :], par[:, w:w + D], xc[:, c * TC + (i % 2) * HC:c * TC + (i % 2 + 1) * HC],
                       start=True, stop=True).then_inc(gate_mm, 1)

            def turn(e):
                pe.wait_ge(gather_in[e], 16 * ST)
                if e >= 2:
                    pe.wait_ge(xg_done, e - 1)
                for i in range(ST):
                    s = e * ST + i
                    last = nc.tensor.transpose(tp[e % 2][:, i * P:(i + 1) * P],
                                               gathered[:, s * D:(s + 1) * D], ident[:, :])
                last.then_inc(xg_tp, 1)

            def up(e):
                pe.wait_ge(xg_done, e + 1)
                if e == 0:
                    pe.wait_ge(w1_in, 16)
                for k in range(KF):
                    n = e * KF + k
                    if n >= 2:
                        pe.wait_ge(h_done, n - 1)
                    mm(hid[n % 2][:, :], w1_sb[:, e * F + k * P:e * F + (k + 1) * P], xgT[:, e % 2, :],
                       start=True, stop=True).then_inc(h_mm, 1)

            def down(e):
                pe.wait_ge(h_done, KF * (e + 1))
                if e == 0:
                    pe.wait_ge(w2_in, 16)
                    pe.wait_ge(idx_done, 2)
                if e >= 1:
                    pe.wait_ge(y_done, e)
                for s in range(ST):
                    for k in range(KF):
                        last = mm(yb[:, s * D:(s + 1) * D], h_sb[:, e % 2, k * CAP + s * P:k * CAP + (s + 1) * P],
                                  w2_sb[:, (e * KF + k) * D:(e * KF + k + 1) * D],
                                  start=(k == 0), stop=(k == KF - 1))
                last.then_inc(y_mm, 1)

            def project(c):
                for half in range(2):
                    n = 2 * c + half
                    pe.wait_ge(scan_done, c + 1)
                    if n >= 3:
                        pe.wait_ge(attn_done, 4 * (n - 2))
                    elif n < 2:
                        pe.wait_ge(gate_free, 4 * C)
                    for i in range(4):
                        j = 4 * half + i
                        last = mm(obank[n % 3][:, i * D:(i + 1) * D], hs[:, c * TC + j:(c + 1) * TC:J],
                                  par[:, WO_T:WO_T + D], start=True, stop=True)
                    last.then_inc(o_mm, 1)

            gates(0)
            turn(0)
            up(0)
            gates(1)
            turn(1)
            up(1)
            down(0)
            gates(2)
            turn(2)
            up(2)
            down(1)
            gates(3)
            turn(3)
            up(3)
            down(2)
            turn(4)
            up(4)
            down(3)
            project(0)
            turn(5)
            up(5)
            project(1)
            down(4)
            project(2)
            turn(6)
            up(6)
            project(3)
            down(5)
            turn(7)
            up(7)
            down(6)
            down(7)

        @block.scalar
        def _(act):
            a = nc.scalar.activation
            act.wait_ge(consts, 3)

            def root(c):
                act.wait_ge(aggr_done, J * (c + 1))
                a(std[:, c * J:(c + 1) * J], mv[:, c * J:(c + 1) * J, 1], ACT.Sqrt,
                  bias=eps[:, 0:1]).then_inc(std_done, 1)

            def untile(n):
                c = n // 2
                act.wait_ge(tp_done, n + 1)
                dst = xnT[:, c * TC:(c + 1) * TC].rearrange("d (p j) -> d j p", j=J)
                a(dst[:, 4 * (n % 2):4 * (n % 2) + 4, :], tp[n % 2][:, :].rearrange("d (j p) -> d j p", j=4),
                  ACT.Copy).then_inc(xnT_done, 1)

            root(0)
            root(1)
            untile(0)
            untile(1)
            root(2)
            untile(2)
            untile(3)
            root(3)
            for n in range(4, 2 * C):
                untile(n)

            nc.scalar.preload_act_table_set("natural_log_exp_and_others")
            act.wait_ge(coef, 1)
            a(lna[:, 1:2], lna[:, 0:1], ACT.Exp, scale=-1.0).then_inc(lna_act, 1)
            act.wait_ge(coef, 3)
            a(lna[:, 4:5], lna[:, 3:4], ACT.Ln).then_inc(lna_act, 1)
            act.wait_ge(shift_done, 1)
            a(shifted[:, :, :], shifted[:, :, :], ACT.Exp).then_inc(exp_done, 1)

            def gates(c):
                if c == 0:
                    act.wait_ge(coef, 6)
                for i, (dst, bias, done) in enumerate(((dec, 0, tanh_r), (dec, 0, tanh_r),
                                                       (inp, 1, tanh_i), (inp, 1, tanh_i))):
                    n = 4 * c + i
                    act.wait_ge(gate_mm, n + 1)
                    o = c * TC + (i % 2) * HC
                    a(dst[:, o:o + HC], gate[n % 2][:, :], ACT.Tanh, bias=half_b[:, bias:bias + 1],
                      scale=0.5).then_inc(gate_free, 1)
                cols = slice(c * TC, (c + 1) * TC)
                act.wait_ge(gate_free, 4 * c + 2)
                a(dec[:, cols], dec[:, cols], ACT.Exp, bias=lna[:, 5:6], scale=lna[:, 5:6]).then_inc(decay_done, 1)
                act.wait_ge(decay_done, c + 1)
                if c == 0:
                    act.wait_ge(table_done, 1)
                a(sca[:, cols], dec[:, cols], ACT.Square).then_inc(square_done, 1)

            def relu(e):
                if e >= 2:
                    act.wait_ge(y_mm, e - 1)
                for k in range(KF):
                    n = e * KF + k
                    act.wait_ge(h_mm, n + 1)
                    a(h_sb[:, e % 2, k * CAP:(k + 1) * CAP], hid[n % 2][:, :], ACT.Relu).then_inc(h_done, 1)

            def scale(c):
                cols = slice(c * TC, (c + 1) * TC)
                act.wait_ge(clip_done, c + 1)
                a(sca[:, cols], sca[:, cols], ACT.Sqrt, bias=quarter).then_inc(scale_done, 1)

            def squares(n):
                act.wait_ge(o_mm, n + 1)
                for i in range(4):
                    t = 4 * n + i
                    if t >= 1:
                        act.wait_ge(ssq_done, t)
                    a(sq[:, :], obank[n % 3][:, i * D:(i + 1) * D], ACT.Square,
                      accum_out=ssq[:, t:t + 1]).then_inc(ssq_done, 1)
                act.wait_ge(ssq_done, 4 * (n + 1))
                a(rms[:, 4 * n:4 * n + 4], ssq[:, 4 * n:4 * n + 4], ACT.Sqrt, bias=eps[:, 1:2],
                  scale=1.0 / D).then_inc(rms_std, 1)

            gates(0)
            relu(0)
            gates(1)
            relu(1)
            gates(2)
            relu(2)
            gates(3)
            relu(3)
            for c in range(C):
                scale(c)
            relu(4)
            squares(0)
            squares(1)
            relu(5)
            squares(2)
            squares(3)
            squares(4)
            squares(5)
            relu(6)
            squares(6)
            squares(7)
            relu(7)

        @block.vector
        def _(dve):
            v = nc.vector

            def moments(c):
                dve.wait_ge(x_in[c], 16)
                for t in range(c * J, (c + 1) * J):
                    v.bn_stats(stats[:, t, :], x_tok[:, t * D:(t + 1) * D]).then_inc(stat_done, 1)
                for t in range(c * J, (c + 1) * J):
                    dve.wait_ge(stat_done, t + 1)
                    v.bn_aggr(mv[:, t, :], stats[:, t, :]).then_inc(aggr_done, 1)

            def normalise(c):
                dve.wait_ge(std_done, c + 1)
                v.reciprocal(rstd[:, c * J:(c + 1) * J], std[:, c * J:(c + 1) * J]).then_inc(rstd_done, 1)
                dve.wait_ge(rstd_done, c + 1)
                dve.wait_ge(aggr_done, J * (c + 1))
                for t in range(c * J, (c + 1) * J):
                    v.tensor_scalar(xn_tok[:, t * D:(t + 1) * D], x_tok[:, t * D:(t + 1) * D], mv[:, t, 0:1],
                                    rstd[:, t:t + 1], ALU.subtract, ALU.mult).then_inc(norm_done, 1)

            moments(0)
            moments(1)
            normalise(0)
            moments(2)
            normalise(1)
            moments(3)
            normalise(2)
            normalise(3)

            dve.wait_ge(par_in, 16)
            log_a = par[:, LOG_A:LOG_A + 1]
            v.tensor_scalar(lna[:, 0:1], log_a, LOGA_FLOOR, None, ALU.max).then_inc(coef, 1)
            dve.wait_ge(lna_act, 1)
            v.tensor_scalar(lna[:, 2:3], lna[:, 1:2], 1.0, None, ALU.add).then_inc(coef, 1)
            dve.wait_ge(coef, 2)
            v.reciprocal(lna[:, 3:4], lna[:, 2:3]).then_inc(coef, 1)
            v.tensor_scalar(lna[:, 6:7], log_a, -LOGA_FLOOR, 0.0, ALU.add, ALU.min).then_inc(coef, 1)
            v.tensor_scalar(half_b[:, :], par[:, BIAS_R:BIAS_I + 1], 0.5, None, ALU.mult).then_inc(coef, 1)
            dve.wait_ge(coef, 5)
            dve.wait_ge(lna_act, 2)
            v.tensor_scalar(lna[:, 5:6], lna[:, 4:5], lna[:, 6:7], 4.0, ALU.add, ALU.mult).then_inc(coef, 1)

            done = [0]

            def step(ins):
                done[0] += 1
                ins.then_inc(route, 1)
                dve.wait_ge(route, done[0])

            def per_tile(ap):
                return ap.unsqueeze(2).to_broadcast([P, NT, E])

            lg = logits.rearrange("p (t e) -> p t e", e=E)
            dve.wait_ge(consts, 10)
            dve.wait_ge(logits_done, 1)
            step(v.tensor_reduce(top[:, :], lg, AX_X, ALU.max))
            v.tensor_tensor(shifted[:, :, :], lg, per_tile(top[:, :]), ALU.subtract).then_inc(shift_done, 1)
            step(v.tensor_tensor(eq[:, :, :], lg, per_tile(top[:, :]), ALU.is_equal))
            step(v.tensor_tensor(eq[:, :, :], eq[:, :, :], desc[:, :, :], ALU.mult))
            step(v.tensor_reduce(best[:, :], eq[:, :, :], AX_X, ALU.max))
            oh = onehot[:, :, :, :].rearrange("p c e j -> p c j e")
            step(v.tensor_tensor(oh, eq[:, :, :].rearrange("p (c j) e -> p c j e", j=J),
                                 best[:, :].rearrange("p (c j) -> p c j", j=J).unsqueeze(3).to_broadcast([P, C, J, E]),
                                 ALU.is_equal))
            v.tensor_tensor_scan(count[:, :, :, :].rearrange("p c e j -> p (c e j)"),
                                 jmask[:, :, :, :].rearrange("p c e j -> p (c e j)"),
                                 onehot[:, :, :, :].rearrange("p c e j -> p (c e j)"), 0.0,
                                 ALU.mult, ALU.add).then_inc(counted, 1)
            dve.wait_ge(counted, 1)
            flat = "p c e j -> p (c e) j"
            step(v.tensor_tensor(wide[:, :, :, :], count[:, :, :, :], e_base[:, :, :, :], ALU.add))
            dve.wait_ge(offsets, 1)
            step(v.tensor_tensor(wide[:, :, :, :].rearrange(flat), wide[:, :, :, :].rearrange(flat),
                                 before.unsqueeze(2).to_broadcast([P, C * E, J]), ALU.add))
            cnt, kept, free, drop, free_before, drop_before, one = (small[:, i, :] for i in range(7))
            step(v.tensor_scalar(kept, totals, float(CAP), None, ALU.min))
            v.tensor_scalar(free, kept, -1.0, float(CAP), ALU.mult, ALU.add).then_inc(route, 1)
            v.tensor_tensor(drop, totals, kept, ALU.subtract).then_inc(route, 1)
            v.memset(small[:, 6:8, :], 1.0).then_inc(route, 1)
            done[0] += 3
            dve.wait_ge(route, done[0])
            v.tensor_tensor_scan(free_before, one, free, 0.0, ALU.mult, ALU.add).then_inc(route, 1)
            v.tensor_tensor_scan(drop_before, one, drop, 0.0, ALU.mult, ALU.add).then_inc(route, 1)
            done[0] += 2
            dve.wait_ge(route, done[0])
            v.tensor_tensor(free_before, free_before, free, ALU.subtract).then_inc(route, 1)
            v.tensor_tensor(drop_before, drop_before, drop, ALU.subtract).then_inc(route, 1)
            done[0] += 2
            chosen = picked[:, :, :, :].rearrange("p c j e -> p (c j) e")
            step(v.tensor_tensor(picked[:, :, :, :], wide[:, :, :, :].rearrange("p c e j -> p c j e"), oh, ALU.mult))
            step(v.tensor_reduce(slot[:, :], chosen, AX_X, ALU.add))
            step(v.scalar_tensor_tensor(rank[:, :], best[:, :], float(CAP), slot[:, :], ALU.mult, ALU.add))
            step(v.tensor_scalar(keep[:, :], rank[:, :], float(E * CAP + CAP), None, ALU.is_lt))
            step(v.tensor_tensor(picked[:, :, :, :], drop_before.unsqueeze(1).unsqueeze(1).to_broadcast([P, C, J, E]),
                                 oh, ALU.mult))
            step(v.tensor_reduce(over[:, :], chosen, AX_X, ALU.add))
            step(v.scalar_tensor_tensor(over[:, :], rank[:, :], -float(E * CAP + CAP), over[:, :], ALU.add, ALU.add))
            step(v.tensor_tensor(eq[:, :, :], per_tile(over[:, :]),
                                 free_before.unsqueeze(1).to_broadcast([P, NT, E]), ALU.is_ge))
            step(v.tensor_tensor(eq[:, :, :], eq[:, :, :], kept.unsqueeze(1).to_broadcast([P, NT, E]), ALU.mult))
            step(v.tensor_reduce(dslot[:, :], eq[:, :, :], AX_X, ALU.add))
            step(v.tensor_tensor(dslot[:, :], dslot[:, :], over[:, :], ALU.add))
            step(v.tensor_tensor(slot[:, :], slot[:, :], dslot[:, :], ALU.subtract))
            step(v.tensor_tensor(slot[:, :], slot[:, :], keep[:, :], ALU.mult))
            step(v.tensor_tensor(slot[:, :], slot[:, :], dslot[:, :], ALU.add))
            step(v.tensor_copy(slot_i[:, :], slot[:, :]))
            step(v.tensor_scalar(hi_i[:, :], slot_i[:, :], 7, None, ALU.logical_shift_right))
            step(v.tensor_scalar(lo_i[:, :], slot_i[:, :], P - 1, None, ALU.bitwise_and))
            step(v.tensor_copy(lo_f[:, :], lo_i[:, :]))
            dve.wait_ge(exp_done, 1)
            step(v.tensor_reduce(psumx[:, :], shifted[:, :, :], AX_X, ALU.add))
            step(v.reciprocal(prob[:, :], psumx[:, :]))
            step(v.tensor_tensor(prob[:, :], prob[:, :], keep[:, :], ALU.mult))

            def per_slot(ap):
                return ap.unsqueeze(2).to_broadcast([P, NT, NS])

            step(v.tensor_tensor(hi_eq[:, :, :], iota_low[:, 0:NS].unsqueeze(1).to_broadcast([P, NT, NS]),
                                 per_slot(hi_i[:, :]), ALU.is_equal))
            v.tensor_tensor(hi_val[:, :, 0, :], hi_eq[:, :, :], per_slot(tok_id[:, :]), ALU.mult).then_inc(hi_done, 1)
            v.tensor_tensor(hi_val[:, :, 1, :], hi_eq[:, :, :], per_slot(prob[:, :]), ALU.mult).then_inc(hi_done, 1)
            for t in range(NT):
                v.tensor_scalar(low_eq[:, t * P:(t + 1) * P], iota_low[:, :], lo_f[:, t:t + 1], None,
                                ALU.is_equal).then_inc(low_done, 1)

            taps = [0]

            def conv(c):
                cols = slice(c * TC, (c + 1) * TC)
                if c == 0:
                    dve.wait_ge(xnT_done, 2 * C)
                src = xnT[:, cols].rearrange("d (s l) -> d s l", l=L)
                dst = xc[:, cols].rearrange("d (s l) -> d s l", l=L)
                v.tensor_scalar(xc[:, cols], xnT[:, cols], par[:, CONV_W + TAPS - 1:CONV_W + TAPS],
                                par[:, CONV_B:CONV_B + 1], ALU.mult, ALU.add).then_inc(conv_tap, 1)
                for back in range(1, TAPS):
                    taps[0] += 1
                    dve.wait_ge(conv_tap, taps[0])
                    k = CONV_W + TAPS - 1 - back
                    v.scalar_tensor_tensor(dst[:, :, back:], src[:, :, 0:L - back], par[:, k:k + 1], dst[:, :, back:],
                                           ALU.mult, ALU.add).then_inc(conv_tap if back < TAPS - 1 else conv_done, 1)

            def clip(c):
                cols = slice(c * TC, (c + 1) * TC)
                dve.wait_ge(square_done, c + 1)
                v.tensor_scalar(sca[:, cols], sca[:, cols], 1.0, -0.25, ALU.min, ALU.mult).then_inc(clip_done, 1)

            def gated(c):
                cols = slice(c * TC, (c + 1) * TC)
                dve.wait_ge(gate_free, 4 * c + 4)
                dve.wait_ge(conv_done, c + 1)
                v.scalar_tensor_tensor(inp[:, cols], inp[:, cols], 1.0, xc[:, cols], ALU.add,
                                       ALU.mult).then_inc(gated_done, 1)

            def recur(c):
                cols = slice(c * TC, (c + 1) * TC)
                dve.wait_ge(scale_done, c + 1)
                dve.wait_ge(gated_done, c + 1)
                v.tensor_tensor(inp[:, cols], inp[:, cols], sca[:, cols], ALU.mult).then_inc(input_done, 1)
                dve.wait_ge(input_done, c + 1)
                for s in range(SC):
                    o = c * TC + s * L
                    last = v.tensor_tensor_scan(hs[:, o:o + L], dec[:, o:o + L], inp[:, o:o + L], 0.0,
                                                ALU.mult, ALU.add)
                last.then_inc(scan_done, 1)

            def columns(e):
                dve.wait_ge(xg_tp, e + 1)
                if e >= 2:
                    dve.wait_ge(h_mm, KF * (e - 1))
                v.tensor_copy(xgT[:, e % 2, :], tp[e % 2][:, :]).then_inc(xg_done, 1)

            def weigh(e):
                dve.wait_ge(y_mm, e + 1)
                s = slice(e * ST * D, (e + 1) * ST * D)
                v.tensor_tensor(gathered[:, s].rearrange("p (s d) -> p s d", d=D),
                                yb[:, :].rearrange("p (s d) -> p s d", d=D),
                                p_slot[:, e * ST:(e + 1) * ST].unsqueeze(2).to_broadcast([P, ST, D]),
                                ALU.mult).then_inc(y_done, 1)

            def rows(n):
                dve.wait_ge(rms_std, n + 1)
                if n == 0:
                    dve.wait_ge(gam_in, 16)
                    dve.wait_ge(xn_out, 16 * C)
                v.reciprocal(rms[:, 4 * n:4 * n + 4], rms[:, 4 * n:4 * n + 4]).then_inc(rms_done, 1)
                dve.wait_ge(rms_done, n + 1)
                for i in range(4):
                    t = 4 * n + i
                    v.scalar_tensor_tensor(attn[:, t * D:(t + 1) * D], obank[n % 3][:, i * D:(i + 1) * D],
                                           rms[:, t:t + 1], gam[:, :], ALU.mult, ALU.mult).then_inc(attn_done, 1)

            conv(0)
            dve.wait_ge(table_done, 1)
            v.tensor_copy(idx[:, :], table[:, 0:NS]).then_inc(idx_done, 1)
            v.tensor_copy(p_slot[:, :], table[:, NS:2 * NS]).then_inc(idx_done, 1)
            columns(0)
            conv(1)
            clip(0)
            gated(0)
            columns(1)
            conv(2)
            weigh(0)
            clip(1)
            gated(1)
            columns(2)
            conv(3)
            weigh(1)
            clip(2)
            gated(2)
            columns(3)
            clip(3)
            gated(3)
            weigh(2)
            columns(4)
            recur(0)
            weigh(3)
            recur(1)
            columns(5)
            recur(2)
            recur(3)
            rows(0)
            rows(1)
            weigh(4)
            rows(2)
            columns(6)
            rows(3)
            rows(4)
            weigh(5)
            rows(5)
            columns(7)
            rows(6)
            rows(7)
            weigh(6)
            weigh(7)


def kernel(**inputs):
    import numpy as _np
    import concourse.bacc as _bacc
    from concourse.bass_utils import run_bass_kernel_spmd as _run

    a = {k[3:]: _np.ascontiguousarray(v) for k, v in inputs.items()}
    params = _np.concatenate([
        a["attn_W_r"].T, a["attn_W_i"].T, a["attn_W_out"].T, a["ffn_Wr"],
        a["attn_conv_w"].reshape(D, TAPS), a["attn_conv_b"].reshape(D, 1), a["attn_b_r"].reshape(D, 1),
        a["attn_b_i"].reshape(D, 1), a["attn_log_a"].reshape(D, 1)], axis=1)
    arrays = {
        "in_x": a["attn_x"],
        "in_params": _np.ascontiguousarray(params),
        "in_gamma": a["attn_gamma"],
        "in_w1": _np.ascontiguousarray(a["ffn_W1"].transpose(1, 0, 2).reshape(P, E * F)),
        "in_w2": _np.ascontiguousarray(a["ffn_W2"].reshape(E, KF, P, D).transpose(2, 0, 1, 3).reshape(P, E * KF * D)),
    }
    nc = _bacc.Bacc("TRN2", target_bir_lowering=False, num_devices=1)
    args = [nc.dram_tensor(n, v.shape, mybir.dt.from_np(v.dtype), kind="ExternalInput").ap()
            for n, v in arrays.items()]
    xn_rows = nc.dram_tensor("xn_rows", (T, D), F32, kind="Internal").ap()
    out = nc.dram_tensor("out_0", (B, L, D), F32, kind="ExternalOutput").ap()
    rglru_moe_kernel(nc, *args, xn_rows, out)
    r = _run(nc, [arrays], core_ids=[0])
    return r.results[0]["out_0"]
```

```python
from contextlib import ExitStack

import concourse.bass as bass
from concourse import mybir

F32 = mybir.dt.float32
I32 = mybir.dt.int32
F16 = mybir.dt.float16
BF16 = mybir.dt.bfloat16
ALU = mybir.AluOpType
ACT = mybir.ActivationFunctionType
AX_X = mybir.AxisListType.X

P = 128
B, L, D = 16, 256, 128
T = B * L
E, F = 8, 512
CAP = T // E
C = 4
J = T // C // P
NT = C * J
TC = T // C
SC = TC // L
HC = TC // 2
KF = F // P
ST = CAP // P
NS = E * ST
TAPS = 4
Q = P // C
NB = TC // Q
PARTS = 3
PART_STEP = 2.0 ** 11
LN_EPS = 1e-5
RMS_EPS = 1e-6
LOGA_FLOOR = -20.0

WR_T, WI_T, WO_T = 0, D, 2 * D
ROUTER = 3 * D
CONV_W = ROUTER + E
CONV_B, BIAS_R, BIAS_I, LOG_A = (CONV_W + TAPS + i for i in range(4))
NPAR = LOG_A + 1


def rglru_moe_kernel(nc, x, params, gamma, w1, w2, xn_rows, out):
    x_rows = x.rearrange("b l d -> (b l) d")
    out_rows = out.rearrange("b l d -> (b l) d")

    def chunk_rows(dram, c):
        return dram[c * TC:(c + 1) * TC, :].rearrange("(p j) d -> p (j d)", p=P)

    with ExitStack() as ctx:
        def sb(name, shape, dt=F32):
            return ctx.enter_context(nc.sbuf_tensor(name, shape, dt))

        def psum(name):
            return ctx.enter_context(nc.psum_tensor(name, [P, 512], F32))

        def sem(name):
            return ctx.enter_context(nc.semaphore(name))

        par = sb("par", [P, NPAR])
        gam = sb("gam", [P, D])
        w1_sb = sb("w1_sb", [P, E * F])
        w2_sb = sb("w2_sb", [P, E * KF * D])
        x_tok = sb("x_tok", [P, NT * D])
        xn_tok = sb("xn_tok", [P, NT * D])
        xnT = sb("xnT", [P, T])
        xc = sb("xc", [P, T])
        dec = sb("dec", [P, T])
        inp = sb("inp", [P, T])
        sca = sb("sca", [P, T])
        h_sb = sb("h_sb", [P, 2, KF * CAP])
        xgT = sb("xgT", [P, 2, CAP])
        ident = sb("ident", [P, P])
        same_q = sb("same_q", [P, P], BF16)
        below = sb("below", [P, P], BF16)
        earlier_q = sb("earlier_q", [P, P], BF16)
        ones = sb("ones", [P, P], BF16)
        diag = sb("diag", [P, TAPS, P])
        iota_tok = sb("iota_tok", [P, NB])
        chunk_of = sb("chunk_of", [P, 1])
        tok_id = sb("tok_id", [P, NB], F16)
        ecap = sb("ecap", [P, E])
        emask = sb("emask", [P, NB, E])
        bmask = sb("bmask", [P, E, NB])
        eps = sb("eps", [P, 3])
        quarter = eps[:, 2:3]
        stats = sb("stats", [P, NT, 6])
        mv = sb("mv", [P, NT, 2])
        std = sb("std", [P, NT])
        rstd = sb("rstd", [P, NT])
        nmr = sb("nmr", [P, NT])
        half_b = sb("half_b", [P, 2])
        lna = sb("lna", [P, 8])
        top = sb("top", [P, NB])
        eq = sb("eq", [P, NB, E])
        nth = sb("nth", [P, NB, E])
        shifted = sb("shifted", [P, NB, E])
        onehot = sb("onehot", [P, E, NB], BF16)
        in_row = sb("in_row", [P, E])
        in_row16 = sb("in_row16", [P, E], BF16)
        blocks = sb("blocks", [P, E, NB])
        picked = sb("picked", [P, E, NB])
        first = sb("first", [P, NB])
        rank = sb("rank", [P, NB])
        keep = sb("keep", [P, NB])
        slot = sb("slot", [P, NB])
        over = sb("over", [P, NB])
        dslot = sb("dslot", [P, NB])
        small = sb("small", [P, 8, E])
        slot_i = sb("slot_i", [P, NB], I32)
        hi_i = sb("hi_i", [P, NB], I32)
        lo_i = sb("lo_i", [P, NB], I32)
        lo16 = sb("lo16", [P, NB], F16)
        hi16 = sb("hi16", [P, NB], F16)
        hi_eq = sb("hi_eq", [P, NS, NB], F16)
        hi_val = sb("hi_val", [P, NS, NB], F16)
        prob = sb("prob", [P, NB])
        part = sb("part", [P, PARTS, NB], F16)
        rest = sb("rest", [P, PARTS, NB])
        idx = sb("idx", [P, NS], I32)
        p_slot = sb("p_slot", [P, NS])
        p_sum = sb("p_sum", [P, NS])
        sq = sb("sq", [P, D])
        ssq = sb("ssq", [P, NT])
        rms = sb("rms", [P, NT])
        yT = sb("yT", [P, CAP])
        lgT = h_sb[:, 0, 0:C * NB * E]
        low_eq = h_sb[:, 1, :].bitcast(F16).rearrange("p (v b) -> p v b", b=NB)
        hi_part = xn_tok[:, 0:NB * PARTS * NS // 2].bitcast(F16).rearrange("p (k s b) -> p k s b", k=PARTS, s=NS)
        values = inp[:, 2 * TC:4 * TC].bitcast(F16).rearrange("p (v b) -> p v b", b=NB)
        hs = xnT
        gathered = x_tok
        attn = xn_tok

        tp = [psum("tp0"), psum("tp1")]
        gate = [psum("gate0"), psum("gate1")]
        hid = [psum("hid0"), psum("hid1")]
        two = ctx.enter_context(nc.psum_tensor("two", [P, 2 * HC], F32))
        yb, tb = two[:, 0:HC], two[:, HC:2 * HC]
        in_block = yb[:, 0:E * NB]
        before = tb[:, 0:E * NB]
        totals = tb[:, E * NB:E * NB + E]
        table = yb[:, 0:NS]
        p_table = yb[:, NS:NS + PARTS * NS]
        obank = gate

        x_in = [sem(f"x_in{c}") for c in range(C)]
        par_in = sem("par_in")
        gam_in = sem("gam_in")
        w1_in = sem("w1_in")
        w2_in = sem("w2_in")
        x_out = sem("x_out")
        xn_out = sem("xn_out")
        consts = sem("consts")
        fill = sem("fill")
        stat_done = sem("stat_done")
        aggr_done = sem("aggr_done")
        std_done = sem("std_done")
        rstd_done = sem("rstd_done")
        norm_done = sem("norm_done")
        tp_done = sem("tp_done")
        xnT_done = sem("xnT_done")
        logits_done = sem("logits_done")
        psum_clear = sem("psum_clear")
        valued = sem("valued")
        chunked = sem("chunked")
        nmr_done = sem("nmr_done")
        norm_act = sem("norm_act")
        norm_pool = sem("norm_pool")
        diag_done = sem("diag_done")
        conv_mm = sem("conv_mm")
        route = sem("route")
        onehot_done = sem("onehot_done")
        row_done = sem("row_done")
        in_block_done = sem("in_block_done")
        before_done = sem("before_done")
        shift_done = sem("shift_done")
        exp_done = sem("exp_done")
        hi_done = sem("hi_done")
        low_done = sem("low_done")
        table_done = sem("table_done")
        idx_done = sem("idx_done")
        parts_done = sem("parts_done")
        hi_part_done = sem("hi_part_done")
        p_table_done = sem("p_table_done")
        p_slot_done = sem("p_slot_done")
        yT_mm = sem("yT_mm")
        yT_done = sem("yT_done")
        coef = sem("coef")
        lna_act = sem("lna_act")
        conv_done = sem("conv_done")
        conv_tap = sem("conv_tap")
        conv_dve = sem("conv_dve")
        conv_pool = sem("conv_pool")
        tap_done = sem("tap_done")
        gate_mm = sem("gate_mm")
        gate_free = sem("gate_free")
        tanh_r = sem("tanh_r")
        tanh_i = sem("tanh_i")
        decay_done = sem("decay_done")
        square_done = sem("square_done")
        clip_done = sem("clip_done")
        scale_done = sem("scale_done")
        gated_done = sem("gated_done")
        input_done = sem("input_done")
        scan_done = sem("scan_done")
        o_mm = sem("o_mm")
        ssq_done = sem("ssq_done")
        rms_std = sem("rms_std")
        rms_done = sem("rms_done")
        attn_done = sem("attn_done")
        gather_in = [sem(f"gather_in{e}") for e in range(E)]
        xg_tp = sem("xg_tp")
        xg_done = sem("xg_done")
        h_mm = sem("h_mm")
        h_done = sem("h_done")
        y_mm = sem("y_mm")
        y_done = sem("y_done")
        scattered = sem("scattered")
        attn_out = sem("attn_out")

        block = ctx.enter_context(nc.Block())

        DVE_TILES = [(0,)] * (C - 1) + [(0, 1, 4, 5)]
        ACT_TILES = [(1, 4, 5)] * (C - 1) + [(2, 6)]
        POOL_TILES = [(2, 3, 6, 7)] * (C - 1) + [(3, 7)]

        def normalised(eng, c, half):
            for done, tiles in ((norm_done, DVE_TILES), (norm_act, ACT_TILES), (norm_pool, POOL_TILES)):
                eng.wait_ge(done, sum(len(js) for js in tiles[:c]) + sum(j < 4 * (half + 1) for j in tiles[c]))

        BEFORE_ATTN = 5

        @block.sync
        def _(sp):
            for c in range(C):
                sp.dma_start(x_tok[:, c * J * D:(c + 1) * J * D], chunk_rows(x_rows, c)).then_inc(x_in[c], 16)
            for c in range(C):
                normalised(sp, c, 1)
                sp.dma_start(chunk_rows(xn_rows, c), xn_tok[:, c * J * D:(c + 1) * J * D]).then_inc(xn_out, 16)
                sp.wait_ge(x_in[c], 16)
                sp.dma_start(chunk_rows(out_rows, c), x_tok[:, c * J * D:(c + 1) * J * D]).then_inc(x_out, 16)
            sp.dma_start(w1_sb[:, :], w1).then_inc(w1_in, 16)
            sp.dma_start(w2_sb[:, :], w2).then_inc(w2_in, 16)

        EARLY_CONSTS = 3 + 1 + 4
        CONSTS = EARLY_CONSTS + 3

        POOL_CONV, PE_CONV = 2, 2

        GATE_ORDER = (0, 2, 1, 3)

        def gate_count(c):
            return 4 * GATE_ORDER.index(c)

        def convolved(eng, c, half):
            if c < POOL_CONV:
                eng.wait_ge(conv_pool, (TAPS - 1) * (c + 1))
            elif 2 * c < 2 * POOL_CONV + PE_CONV:
                eng.wait_ge(conv_done, 2 * (c - POOL_CONV) + half + 1)
            else:
                eng.wait_ge(conv_dve, c - POOL_CONV - PE_CONV // 2 + 1)

        GATES_AFTER = {0: (3,)}
        DECAY_AT = {0: (0, 1), 1: (2, 3)}
        SCALE_AT = {2: (0, 1), 3: (2, 3)}
        PROJECT_AT = {3: (1,), 4: (4,), 5: (6,)}
        PROJECT_AFTER = {2: (0,), 3: (2, 3), 4: (5,), 5: (7,)}

        @block.gpsimd
        def _(pool):
            g = nc.gpsimd
            g.memset(eps[:, 0:1], LN_EPS).then_inc(consts, 1)
            g.memset(eps[:, 1:2], RMS_EPS).then_inc(consts, 1)
            g.memset(eps[:, 2:3], 0.25).then_inc(consts, 1)
            exact = dict(allow_small_or_imprecise_dtypes=True)
            in_q = [[-Q, C], [0, Q]]
            g.memset(ident[:, :], 0.0).then_inc(fill, 1)
            g.memset(ones[:, :], 1.0).then_inc(fill, 1)
            g.memset(emask[:, :, :], 1.0).then_inc(fill, 1)
            g.memset(bmask[:, :, :], 1.0).then_inc(fill, 1)
            pool.wait_ge(fill, 1)
            g.affine_select(out=ident[:, :], in_=ident[:, :], compare_op=ALU.not_equal, fill=1.0, base=0,
                            pattern=[[-1, P]], channel_multiplier=1).then_inc(consts, 1)

            def normalise(c):
                pool.wait_ge(nmr_done, c + 1)
                for j in POOL_TILES[c]:
                    t = c * J + j
                    g.tensor_scalar(xn_tok[:, t * D:(t + 1) * D], x_tok[:, t * D:(t + 1) * D], rstd[:, t:t + 1],
                                    nmr[:, t:t + 1], ALU.mult, ALU.add).then_inc(norm_pool, 1)

            pool.wait_ge(fill, 4)
            g.memset(emask[:, :, 0:1], 0.0).then_inc(consts, 1)
            g.memset(bmask[:, :, 0:1], 0.0).then_inc(consts, 1)
            g.iota(ecap[:, :], [[CAP, E]], base=0, channel_multiplier=0, **exact).then_inc(consts, 1)
            g.iota(iota_tok[:, :], [[Q, NB]], base=-T // 2, channel_multiplier=1, **exact).then_inc(consts, 1)
            g.iota(values, [[1, P], [0, NB]], base=0, channel_multiplier=0, **exact).then_inc(valued, 1)
            normalise(0)
            g.affine_select(out=same_q[:, :], in_=ones[:, :], compare_op=ALU.is_ge, fill=0.0, base=0,
                            pattern=in_q, channel_multiplier=1).then_inc(fill, 1)
            g.affine_select(out=earlier_q[:, :], in_=ones[:, :], compare_op=ALU.is_gt, fill=0.0, base=0,
                            pattern=[[Q, C], [0, Q]], channel_multiplier=-1).then_inc(consts, 1)
            normalise(1)
            pool.wait_ge(fill, 5)
            g.affine_select(out=same_q[:, :], in_=same_q[:, :], compare_op=ALU.is_ge, fill=0.0, base=Q - 1,
                            pattern=[[Q, C], [0, Q]], channel_multiplier=-1).then_inc(consts, 1)
            pool.wait_ge(consts, CONSTS - 1)
            g.tensor_scalar(below[:, :], same_q[:, :], -1.0, 0.0, ALU.mult, ALU.add).then_inc(fill, 1)
            pool.wait_ge(fill, 6)
            g.affine_select(out=below[:, :], in_=below[:, :], compare_op=ALU.is_ge, fill=0.0, base=0,
                            pattern=[[-1, P]], channel_multiplier=1).then_inc(consts, 1)
            normalise(2)
            added = [0]

            def conv(c):
                dst = xc[:, c * TC:(c + 1) * TC].rearrange("d (s l) -> d s l", l=L)
                for back in range(1, TAPS):
                    src = sca[:, back * TC:(back + 1) * TC].rearrange("d (s l) -> d s l", l=L)
                    pool.wait_ge(tap_done, TAPS * c + back + 1)
                    if back > 1:
                        pool.wait_ge(conv_pool, added[0])
                    added[0] += 1
                    g.tensor_tensor(dst[:, :, back:], dst[:, :, back:], src[:, :, 0:L - back],
                                    ALU.add).then_inc(conv_pool, 1)

            normalise(3)
            for c in range(POOL_CONV):
                conv(c)
            def gather(e):
                for s in range(e * ST, (e + 1) * ST):
                    g.indirect_dma_start(gathered[:, s * D:(s + 1) * D], None, xn_rows,
                                         bass.IndirectOffsetOnAxis(ap=idx[:, s:s + 1], axis=0)
                                         ).then_inc(gather_in[e], 16)

            def scatter(e):
                pool.wait_ge(y_done, e + 1)
                for s in range(e * ST, (e + 1) * ST):
                    g.indirect_dma_start(out_rows, bass.IndirectOffsetOnAxis(ap=idx[:, s:s + 1], axis=0),
                                         gathered[:, s * D:(s + 1) * D], None,
                                         compute_op=ALU.add).then_inc(scattered, 16)

            pool.wait_ge(xn_out, 16 * C)
            pool.wait_ge(x_out, 16 * C)
            pool.wait_ge(idx_done, 1)
            for e in range(4):
                gather(e)
            for e in range(4, E):
                scatter(e - 4)
                gather(e)
            for e in range(4, BEFORE_ATTN):
                scatter(e)
            pool.wait_ge(scattered, 16 * ST * BEFORE_ATTN)
            for c in range(C):
                pool.wait_ge(attn_done, J * (c + 1))
                g.dma_start(chunk_rows(out_rows, c), attn[:, c * J * D:(c + 1) * J * D],
                            accum_op=ALU.add).then_inc(attn_out, 16)
            pool.wait_ge(attn_out, 16 * C)
            for e in range(BEFORE_ATTN, E):
                scatter(e)
            pool.wait_ge(scattered, 16 * NS)

        @block.tensor
        def _(pe):
            mm = nc.tensor.matmul
            pe.wait_ge(consts, 4)

            def router(n):
                c, half = n // 2, n % 2
                if n == 0:
                    pe.wait_ge(par_in, 16)
                    pe.wait_ge(psum_clear, 1)
                pe.wait_ge(xnT_done, 2 * (c + 1))
                return mm(two[c * Q:c * Q + E, half * HC:(half + 1) * HC], par[:, ROUTER:ROUTER + E],
                          xnT[:, c * TC + half * HC:c * TC + (half + 1) * HC], start=True, stop=True)

            for n in range(2 * C):
                normalised(pe, n // 2, n % 2)
                if n >= 2:
                    pe.wait_ge(xnT_done, n - 1)
                for i in range(4):
                    t = 4 * n + i
                    last = nc.tensor.transpose(tp[n % 2][:, i * P:(i + 1) * P],
                                               xn_tok[:, t * D:(t + 1) * D], ident[:, :])
                last.then_inc(tp_done, 1)
                if n % 2 == 1 and n > 1:
                    router(n - 3)
                    router(n - 2)
            router(2 * C - 2)
            router(2 * C - 1).then_inc(logits_done, 1)

            def conv(i):
                n = 2 * POOL_CONV + i
                if i == 0:
                    pe.wait_ge(diag_done, TAPS)
                elif i >= 2:
                    pe.wait_ge(conv_done, i - 1)
                cols = slice(n * HC, (n + 1) * HC)
                src = xnT[:, cols].rearrange("d (s l) -> d s l", l=L)
                dst = hid[i % 2][:, :].rearrange("d (s l) -> d s l", l=L)
                mm(hid[i % 2][:, :], diag[:, TAPS - 1, :], xnT[:, cols], start=True, stop=False)
                for back in range(1, TAPS):
                    last = mm(dst[:, :, back:], diag[:, TAPS - 1 - back, :], src[:, :, 0:L - back],
                              start=False, stop=(back == TAPS - 1))
                last.then_inc(conv_mm, 1)

            def gate_half(c, i):
                n = gate_count(c) + i
                convolved(pe, c, i % 2)
                if n >= 2:
                    pe.wait_ge(gate_free, n - 1)
                w = WR_T if i < 2 else WI_T
                mm(gate[n % 2][:, :], par[:, w:w + D], xc[:, c * TC + (i % 2) * HC:c * TC + (i % 2 + 1) * HC],
                   start=True, stop=True).then_inc(gate_mm, 1)

            def gates(c):
                for i in range(4):
                    gate_half(c, i)

            conv(0)
            pe.wait_ge(consts, CONSTS)
            pe.wait_ge(onehot_done, 1)
            oh = onehot[:, :, :].rearrange("p e b -> p (e b)")
            mm(in_block, same_q[:, :], oh, start=True, stop=True).then_inc(in_block_done, 1)
            mm(before, below[:, :], oh, start=True, stop=False)
            pe.wait_ge(row_done, 1)
            mm(before, earlier_q[:, :], in_row16[:, :].unsqueeze(2).to_broadcast([P, E, NB]), start=False, stop=True)
            mm(totals, ones[:, :], in_row16[:, :], start=True, stop=True).then_inc(before_done, 1)
            conv(1)
            gates(0)

            pe.wait_ge(hi_done, 1)
            for b in range(NB):
                pe.wait_ge(low_done, b // (NB // 2) + 1)
                last = mm(table, low_eq[:, :, b], hi_val[:, :, b], start=(b == 0), stop=(b == NB - 1))
            last.then_inc(table_done, 1)

            def p_pass():
                pe.wait_ge(hi_part_done, PARTS)
                for b in range(NB):
                    last = mm(p_table, low_eq[:, :, b], hi_part[:, :, :, b],
                              start=(b == 0), stop=(b == NB - 1))
                last.then_inc(p_table_done, 1)

            def turn(e):
                pe.wait_ge(gather_in[e], 16 * ST)
                if e >= 2:
                    pe.wait_ge(xg_done, e - 1)
                for i in range(ST):
                    s = e * ST + i
                    last = nc.tensor.transpose(tp[e % 2][:, i * P:(i + 1) * P],
                                               gathered[:, s * D:(s + 1) * D], ident[:, :])
                last.then_inc(xg_tp, 1)

            def up(e):
                pe.wait_ge(xg_done, e + 1)
                if e == 0:
                    pe.wait_ge(w1_in, 16)
                    pe.wait_ge(conv_done, PE_CONV)
                for k in range(KF):
                    n = e * KF + k
                    if n >= 2:
                        pe.wait_ge(h_done, n - 1)
                    mm(hid[n % 2][:, :], w1_sb[:, e * F + k * P:e * F + (k + 1) * P], xgT[:, e % 2, :],
                       start=True, stop=True).then_inc(h_mm, 1)

            def down(e):
                pe.wait_ge(h_done, KF * (e + 1))
                if e == 0:
                    pe.wait_ge(w2_in, 16)
                    pe.wait_ge(hi_done, 1)
                else:
                    pe.wait_ge(yT_done, e)
                for k in range(KF):
                    last = mm(tb, w2_sb[:, (e * KF + k) * D:(e * KF + k + 1) * D],
                              h_sb[:, e % 2, k * CAP:(k + 1) * CAP], start=(k == 0), stop=(k == KF - 1))
                last.then_inc(yT_mm, 1)

            def back(e):
                pe.wait_ge(yT_done, e + 1)
                if e == 0:
                    pe.wait_ge(p_slot_done, 1)
                else:
                    pe.wait_ge(y_done, e)
                for s in range(ST):
                    last = nc.tensor.transpose(yb[:, s * D:(s + 1) * D], yT[:, s * P:(s + 1) * P], ident[:, :])
                last.then_inc(y_mm, 1)

            def project(n):
                c = n // 2
                pe.wait_ge(scan_done, c + 1)
                if n >= 2:
                    pe.wait_ge(attn_done, 4 * (n - 1))
                else:
                    pe.wait_ge(gate_free, 4 * C)
                for i in range(4):
                    j = 4 * (n % 2) + i
                    last = mm(obank[n % 2][:, i * D:(i + 1) * D], hs[:, c * TC + j:(c + 1) * TC:J],
                              par[:, WO_T:WO_T + D], start=True, stop=True)
                last.then_inc(o_mm, 1)

            gates(2)
            gates(1)
            turn(0)
            p_pass()
            up(0)
            for e in range(E):
                if e + 1 < E:
                    turn(e + 1)
                down(e)
                for n in PROJECT_AT.get(e, ()):
                    project(n)
                if e + 1 < E:
                    up(e + 1)
                back(e)
                for c in GATES_AFTER.get(e, ()):
                    gates(c)
                for n in PROJECT_AFTER.get(e, ()):
                    project(n)

        @block.scalar
        def _(act):
            a = nc.scalar.activation
            act.dma_start(par[:, :], params).then_inc(par_in, 16)
            act.dma_start(gam[:, :], gamma.partition_broadcast(P)).then_inc(gam_in, 16)

            def root(c):
                if c == 0:
                    act.wait_ge(consts, 3)
                act.wait_ge(aggr_done, J * (c + 1))
                a(std[:, c * J:(c + 1) * J], mv[:, c * J:(c + 1) * J, 1], ACT.Sqrt,
                  bias=eps[:, 0:1]).then_inc(std_done, 1)

            def normalise(c):
                act.wait_ge(nmr_done, c + 1)
                for j in ACT_TILES[c]:
                    t = c * J + j
                    a(xn_tok[:, t * D:(t + 1) * D], x_tok[:, t * D:(t + 1) * D], ACT.Identity,
                      scale=rstd[:, t:t + 1], bias=nmr[:, t:t + 1]).then_inc(norm_act, 1)

            def untile(n):
                c = n // 2
                act.wait_ge(tp_done, n + 1)
                dst = xnT[:, c * TC:(c + 1) * TC].rearrange("d (p j) -> d j p", j=J)
                a(dst[:, 4 * (n % 2):4 * (n % 2) + 4, :], tp[n % 2][:, :].rearrange("d (j p) -> d j p", j=4),
                  ACT.Copy).then_inc(xnT_done, 1)

            def tap(c, back):
                src = xnT[:, c * TC:(c + 1) * TC]
                k = CONV_W + TAPS - 1 - back
                if c == 0 and back == 0:
                    act.wait_ge(par_in, 16)
                if back == 0:
                    act.wait_ge(xnT_done, 2 * (c + 1))
                    ins = a(xc[:, c * TC:(c + 1) * TC], src, ACT.Identity, scale=par[:, k:k + 1],
                            bias=par[:, CONV_B:CONV_B + 1])
                else:
                    if c >= 1:
                        act.wait_ge(conv_pool, (TAPS - 1) * (c - 1) + back)
                    ins = a(sca[:, back * TC:(back + 1) * TC], src, ACT.Identity, scale=par[:, k:k + 1])
                ins.then_inc(tap_done, 1)

            nc.scalar.preload_act_table_set("natural_log_exp_and_others")
            act.wait_ge(coef, 1)
            a(lna[:, 1:2], lna[:, 0:1], ACT.Exp, scale=-1.0).then_inc(lna_act, 1)
            act.wait_ge(coef, 3)
            a(lna[:, 4:5], lna[:, 3:4], ACT.Ln).then_inc(lna_act, 1)
            nc.scalar.preload_act_table_set("sqrt_and_others")

            root(0)
            normalise(0)
            for c in range(1, C):
                root(c)
                if c == C - 1:
                    tap(0, 0)
                untile(2 * c - 2)
                untile(2 * c - 1)
                normalise(c)
            untile(2 * C - 2)
            untile(2 * C - 1)
            nc.scalar.preload_act_table_set("exp_and_others")

            def biased(i):
                act.wait_ge(conv_mm, i + 1)
                n = 2 * POOL_CONV + i
                a(xc[:, n * HC:(n + 1) * HC], hid[i % 2][:, :], ACT.Identity,
                  bias=par[:, CONV_B:CONV_B + 1]).then_inc(conv_done, 1)

            def gates(c):
                if c == 0:
                    act.wait_ge(coef, 7)
                for i, (dst, bias) in enumerate(((dec, 0), (dec, 0), (inp, 1), (inp, 1))):
                    n = gate_count(c) + i
                    act.wait_ge(gate_mm, n + 1)
                    if c == 2 and i == 2:
                        act.wait_ge(low_done, 2)
                    o = c * TC + (i % 2) * HC
                    a(dst[:, o:o + HC], gate[n % 2][:, :], ACT.Tanh, bias=half_b[:, bias:bias + 1],
                      scale=0.5).then_inc(gate_free, 1)

            def decay(c):
                cols = slice(c * TC, (c + 1) * TC)
                act.wait_ge(gate_free, gate_count(c) + 2)
                a(dec[:, cols], dec[:, cols], ACT.Exp, bias=lna[:, 5:6], scale=lna[:, 5:6]).then_inc(decay_done, 1)
                act.wait_ge(decay_done, c + 1)
                act.wait_ge(conv_pool, (TAPS - 1) * POOL_CONV)
                a(sca[:, cols], dec[:, cols], ACT.Square).then_inc(square_done, 1)

            def relu(e):
                if e == 1:
                    act.wait_ge(p_table_done, 1)
                if e >= 2:
                    act.wait_ge(yT_mm, e - 1)
                for k in range(KF):
                    n = e * KF + k
                    act.wait_ge(h_mm, n + 1)
                    a(h_sb[:, e % 2, k * CAP:(k + 1) * CAP], hid[n % 2][:, :], ACT.Relu).then_inc(h_done, 1)

            def scale(c):
                cols = slice(c * TC, (c + 1) * TC)
                act.wait_ge(clip_done, c + 1)
                a(sca[:, cols], sca[:, cols], ACT.Sqrt, bias=quarter).then_inc(scale_done, 1)

            def squares(n):
                act.wait_ge(o_mm, n + 1)
                for i in range(4):
                    t = 4 * n + i
                    if t >= 1:
                        act.wait_ge(ssq_done, t)
                    a(sq[:, :], obank[n % 2][:, i * D:(i + 1) * D], ACT.Square,
                      accum_out=ssq[:, t:t + 1]).then_inc(ssq_done, 1)
                act.wait_ge(ssq_done, 4 * (n + 1))
                a(rms[:, 4 * n:4 * n + 4], ssq[:, 4 * n:4 * n + 4], ACT.Sqrt, bias=eps[:, 1:2],
                  scale=1.0 / D).then_inc(rms_std, 1)

            def columns(e):
                act.wait_ge(xg_tp, e + 1)
                if e >= 2:
                    act.wait_ge(h_mm, KF * (e - 1))
                a(xgT[:, e % 2, :], tp[e % 2][:, :], ACT.Copy).then_inc(xg_done, 1)

            def output(e):
                act.wait_ge(yT_mm, e + 1)
                if e >= 1:
                    act.wait_ge(y_mm, e)
                a(yT[:, :], tb, ACT.Copy).then_inc(yT_done, 1)

            tap(0, 1)
            tap(0, 2)
            tap(0, 3)
            tap(1, 0)
            tap(1, 1)
            biased(0)
            act.wait_ge(shift_done, 1)
            a(shifted[:, :, :], shifted[:, :, :], ACT.Exp).then_inc(exp_done, 1)
            tap(1, 2)
            biased(1)
            gates(0)
            tap(1, 3)
            gates(2)
            gates(1)
            columns(0)
            relu(0)
            for e in range(E):
                if e + 1 < E:
                    columns(e + 1)
                for c in DECAY_AT.get(e, ()):
                    decay(c)
                for c in SCALE_AT.get(e, ()):
                    scale(c)
                output(e)
                for n in PROJECT_AT.get(e, ()):
                    squares(n)
                if e + 1 < E:
                    relu(e + 1)
                for c in GATES_AFTER.get(e, ()):
                    gates(c)
                for n in PROJECT_AFTER.get(e, ()):
                    squares(n)

        @block.vector
        def _(dve):
            v = nc.vector

            for q in range(C):
                v.memset(chunk_of[q * Q:(q + 1) * Q, :], float((TC - Q) * q)).then_inc(chunked, 1)
            v.memset(two[:, :], 0.0).then_inc(psum_clear, 1)
            log_a = par[:, LOG_A:LOG_A + 1]

            def hold():
                dve.wait_ge(par_in, 16)
                v.tensor_scalar(lna[:, 0:1], log_a, LOGA_FLOOR, None, ALU.max).then_inc(coef, 1)

            def add_one():
                dve.wait_ge(lna_act, 1)
                v.tensor_scalar(lna[:, 2:3], lna[:, 1:2], 1.0, None, ALU.add).then_inc(coef, 1)

            def invert():
                dve.wait_ge(coef, 2)
                v.reciprocal(lna[:, 3:4], lna[:, 2:3]).then_inc(coef, 1)

            coefficient = {3: hold, 5: add_one, 6: invert}

            def moments(c):
                dve.wait_ge(x_in[c], 16)
                for t in range(c * J, (c + 1) * J):
                    v.bn_stats(stats[:, t, :], x_tok[:, t * D:(t + 1) * D]).then_inc(stat_done, 1)
                    if t in coefficient:
                        coefficient[t]()
                for t in range(c * J, (c + 1) * J):
                    dve.wait_ge(stat_done, t + 1)
                    v.bn_aggr(mv[:, t, :], stats[:, t, :]).then_inc(aggr_done, 1)

            def normalise(c):
                dve.wait_ge(std_done, c + 1)
                v.reciprocal(rstd[:, c * J:(c + 1) * J], std[:, c * J:(c + 1) * J]).then_inc(rstd_done, 1)
                dve.wait_ge(rstd_done, c + 1)
                cols = slice(c * J, (c + 1) * J)
                v.scalar_tensor_tensor(nmr[:, cols], mv[:, cols, 0], -1.0, rstd[:, cols], ALU.mult,
                                       ALU.mult).then_inc(nmr_done, 1)
                for j in DVE_TILES[c]:
                    t = c * J + j
                    v.tensor_scalar(xn_tok[:, t * D:(t + 1) * D], x_tok[:, t * D:(t + 1) * D], mv[:, t, 0:1],
                                    rstd[:, t:t + 1], ALU.subtract, ALU.mult).then_inc(norm_done, 1)

            moments(0)
            moments(1)
            normalise(0)
            moments(2)
            normalise(1)
            moments(3)
            normalise(2)
            normalise(3)

            dve.wait_ge(consts, 4)
            for k in range(TAPS):
                v.tensor_scalar(diag[:, k, :], ident[:, :], par[:, CONV_W + k:CONV_W + k + 1], None,
                                ALU.mult).then_inc(diag_done, 1)
            v.tensor_scalar(lna[:, 6:7], log_a, -LOGA_FLOOR, 0.0, ALU.add, ALU.min).then_inc(coef, 1)
            v.tensor_scalar(half_b[:, :], par[:, BIAS_R:BIAS_I + 1], 0.5, None, ALU.mult).then_inc(coef, 1)
            dve.wait_ge(coef, 5)
            dve.wait_ge(lna_act, 2)
            v.tensor_scalar(lna[:, 5:6], lna[:, 4:5], lna[:, 6:7], 4.0, ALU.add, ALU.mult).then_inc(coef, 1)
            dve.wait_ge(consts, EARLY_CONSTS)
            dve.wait_ge(chunked, C)
            v.tensor_scalar(tok_id[:, :], iota_tok[:, :], chunk_of[:, 0:1], None, ALU.add).then_inc(coef, 1)
            dve.wait_ge(coef, 7)

            results = [0]

            def put(ins):
                results[0] += 1
                ins.then_inc(route, 1)
                return results[0]

            def need(n):
                dve.wait_ge(route, n)

            def per_token(ap):
                return ap.unsqueeze(2).to_broadcast([P, NB, E])

            def per_token_eb(ap):
                return ap.unsqueeze(1).to_broadcast([P, E, NB])

            def per_expert(ap):
                return ap.unsqueeze(2).to_broadcast([P, E, NB])

            def over_experts(ap):
                return ap.rearrange("p e b -> p b e")

            dve.wait_ge(logits_done, 1)
            need(put(v.transpose(lgT, two[:, :])))
            lg = lgT.rearrange("p (b w) -> p b w", w=Q)[:, :, 0:E]
            need(put(v.tensor_reduce(top[:, :], lg, AX_X, ALU.max)))
            equal = put(v.tensor_tensor(eq[:, :, :], lg, per_token(top[:, :]), ALU.is_equal))
            v.tensor_tensor(shifted[:, :, :], lg, per_token(top[:, :]), ALU.subtract).then_inc(shift_done, 1)
            need(equal)
            need(put(v.tensor_tensor_scan(nth[:, :, :].rearrange("p b e -> p (b e)"),
                                          emask[:, :, :].rearrange("p b e -> p (b e)"),
                                          eq[:, :, :].rearrange("p b e -> p (b e)"), 0.0, ALU.mult, ALU.add)))
            v.scalar_tensor_tensor(over_experts(onehot[:, :, :]), nth[:, :, :], 1.0, eq[:, :, :], ALU.is_equal,
                                   ALU.mult).then_inc(onehot_done, 1)
            dve.wait_ge(onehot_done, 1)
            need(put(v.tensor_reduce(in_row[:, :], onehot[:, :, :], AX_X, ALU.add)))
            v.tensor_copy(in_row16[:, :], in_row[:, :]).then_inc(row_done, 1)
            product = put(v.tensor_tensor(picked[:, :, :], onehot[:, :, :], per_expert(ecap[:, :]), ALU.mult))
            dve.wait_ge(in_block_done, 1)
            counted = put(v.tensor_tensor_scan(blocks[:, :, :].rearrange("p e b -> p (e b)"),
                                               bmask[:, :, :].rearrange("p e b -> p (e b)"),
                                               in_block, 0.0, ALU.mult, ALU.add))
            need(product)
            based = put(v.tensor_reduce(first[:, :], over_experts(picked[:, :, :]), AX_X, ALU.add))
            kept, free, drop, free_before, drop_before, one = (small[:, i, :] for i in range(6))
            unit = put(v.memset(small[:, 5:6, :], 1.0))
            dve.wait_ge(before_done, 1)
            kept_n = put(v.tensor_scalar(kept, totals, float(CAP), None, ALU.min))
            need(counted)
            wide = put(v.tensor_tensor(blocks[:, :, :].rearrange("p e b -> p (e b)"),
                                       blocks[:, :, :].rearrange("p e b -> p (e b)"), before, ALU.add))
            need(kept_n)
            free_n = put(v.tensor_scalar(free, kept, -1.0, float(CAP), ALU.mult, ALU.add))
            drop_n = put(v.tensor_tensor(drop, totals, kept, ALU.subtract))
            need(wide)
            product = put(v.tensor_tensor(picked[:, :, :], blocks[:, :, :], onehot[:, :, :], ALU.mult))
            need(max(free_n, drop_n, unit))
            fsum = put(v.tensor_tensor_scan(free_before, one, free, 0.0, ALU.mult, ALU.add))
            dsum = put(v.tensor_tensor_scan(drop_before, one, drop, 0.0, ALU.mult, ALU.add))
            need(product)
            ranked = put(v.tensor_reduce(rank[:, :], over_experts(picked[:, :, :]), AX_X, ALU.add))
            need(fsum)
            fbefore = put(v.tensor_tensor(free_before, free_before, free, ALU.subtract))
            need(dsum)
            need(put(v.tensor_tensor(drop_before, drop_before, drop, ALU.subtract)))
            need(ranked)
            product = put(v.tensor_tensor(picked[:, :, :], per_expert(drop_before), onehot[:, :, :], ALU.mult))
            kept_tok = put(v.tensor_scalar(keep[:, :], rank[:, :], float(CAP), None, ALU.is_lt))
            need(based)
            slotted = put(v.tensor_tensor(slot[:, :], rank[:, :], first[:, :], ALU.add))
            need(product)
            need(put(v.tensor_reduce(over[:, :], over_experts(picked[:, :, :]), AX_X, ALU.add)))
            need(put(v.scalar_tensor_tensor(over[:, :], rank[:, :], -float(CAP), over[:, :], ALU.add, ALU.add)))
            need(fbefore)
            need(put(v.tensor_tensor(picked[:, :, :], per_token_eb(over[:, :]), per_expert(free_before), ALU.is_ge)))
            need(put(v.tensor_tensor(picked[:, :, :], picked[:, :, :], per_expert(kept), ALU.mult)))
            need(put(v.tensor_reduce(dslot[:, :], over_experts(picked[:, :, :]), AX_X, ALU.add)))
            need(put(v.tensor_tensor(dslot[:, :], dslot[:, :], over[:, :], ALU.add)))
            need(slotted)
            need(put(v.tensor_tensor(slot[:, :], slot[:, :], dslot[:, :], ALU.subtract)))
            need(kept_tok)
            need(put(v.tensor_tensor(slot[:, :], slot[:, :], keep[:, :], ALU.mult)))
            need(put(v.tensor_tensor(slot_i[:, :], slot[:, :], dslot[:, :], ALU.add)))
            low = put(v.tensor_scalar(lo_i[:, :], slot_i[:, :], P - 1, None, ALU.bitwise_and))
            high = put(v.tensor_scalar(hi_i[:, :], slot_i[:, :], 7, None, ALU.logical_shift_right))
            need(low)
            low = put(v.tensor_copy(lo16[:, :], lo_i[:, :]))
            need(high)
            high = put(v.tensor_copy(hi16[:, :], hi_i[:, :]))

            def per_value(ap, n):
                return ap.unsqueeze(1).to_broadcast([P, n, ap.shape[-1]])

            dve.wait_ge(valued, 1)
            need(high)
            need(put(v.tensor_tensor(hi_eq[:, :, :], values[:, 0:NS, :], per_value(hi16[:, :], NS), ALU.is_equal)))
            v.tensor_tensor(hi_val[:, :, :], hi_eq[:, :, :], per_value(tok_id[:, :], NS), ALU.mult).then_inc(hi_done, 1)
            need(low)
            for half in range(2):
                b = slice(half * NB // 2, (half + 1) * NB // 2)
                v.tensor_tensor(low_eq[:, :, b], values[:, :, b], per_value(lo16[:, b], P),
                                ALU.is_equal).then_inc(low_done, 1)

            dve.wait_ge(table_done, 1)
            v.tensor_scalar(idx[:, :], table, float(T // 2), None, ALU.add).then_inc(idx_done, 1)
            dve.wait_ge(exp_done, 1)
            need(put(v.tensor_reduce(top[:, :], shifted[:, :, :], AX_X, ALU.add)))
            need(put(v.reciprocal(prob[:, :], top[:, :])))
            need(put(v.tensor_tensor(rest[:, 0, :], prob[:, :], keep[:, :], ALU.mult)))
            for k in range(PARTS):
                need(put(v.tensor_copy(part[:, k, :], rest[:, k, :])))
                if k + 1 < PARTS:
                    need(put(v.tensor_tensor(rest[:, k + 1, :], rest[:, k, :], part[:, k, :], ALU.subtract)))
                    need(put(v.tensor_scalar(rest[:, k + 1, :], rest[:, k + 1, :], PART_STEP, None, ALU.mult)))

            taps = [0]

            def conv(c):
                cols = slice(c * TC, (c + 1) * TC)
                src = xnT[:, cols].rearrange("d (s l) -> d s l", l=L)
                dst = xc[:, cols].rearrange("d (s l) -> d s l", l=L)
                v.tensor_scalar(xc[:, cols], xnT[:, cols], par[:, CONV_W + TAPS - 1:CONV_W + TAPS],
                                par[:, CONV_B:CONV_B + 1], ALU.mult, ALU.add).then_inc(conv_tap, 1)
                for back in range(1, TAPS):
                    taps[0] += 1
                    dve.wait_ge(conv_tap, taps[0])
                    k = CONV_W + TAPS - 1 - back
                    v.scalar_tensor_tensor(dst[:, :, back:], src[:, :, 0:L - back], par[:, k:k + 1], dst[:, :, back:],
                                           ALU.mult, ALU.add).then_inc(conv_tap if back < TAPS - 1 else conv_dve, 1)

            def high_parts():
                dve.wait_ge(xn_out, 16 * C)
                for k in range(PARTS):
                    v.tensor_tensor(hi_part[:, k, :, :], hi_eq[:, :, :], per_value(part[:, k, :], NS),
                                    ALU.mult).then_inc(hi_part_done, 1)

            def slot_probabilities():
                dve.wait_ge(p_table_done, 1)
                pt = p_table.rearrange("p (k s) -> p k s", s=NS)
                need(put(v.tensor_copy(p_sum[:, :], pt[:, PARTS - 1, :])))
                for k in range(PARTS - 2, -1, -1):
                    ins = v.scalar_tensor_tensor(p_sum[:, :] if k else p_slot[:, :], p_sum[:, :], 1.0 / PART_STEP,
                                                 pt[:, k, :], ALU.mult, ALU.add)
                    if k:
                        need(put(ins))
                    else:
                        ins.then_inc(p_slot_done, 1)
                dve.wait_ge(p_slot_done, 1)

            def clip(c):
                cols = slice(c * TC, (c + 1) * TC)
                dve.wait_ge(square_done, c + 1)
                v.tensor_scalar(sca[:, cols], sca[:, cols], 1.0, -0.25, ALU.min, ALU.mult).then_inc(clip_done, 1)

            def gated(c):
                cols = slice(c * TC, (c + 1) * TC)
                dve.wait_ge(gate_free, gate_count(c) + 4)
                if 2 * c < 2 * POOL_CONV + PE_CONV:
                    convolved(dve, c, 1)
                v.scalar_tensor_tensor(inp[:, cols], inp[:, cols], 1.0, xc[:, cols], ALU.add,
                                       ALU.mult).then_inc(gated_done, 1)

            def recur(c):
                cols = slice(c * TC, (c + 1) * TC)
                dve.wait_ge(scale_done, c + 1)
                dve.wait_ge(gated_done, c + 1)
                v.tensor_tensor(inp[:, cols], inp[:, cols], sca[:, cols], ALU.mult).then_inc(input_done, 1)
                dve.wait_ge(input_done, c + 1)
                for s in range(SC):
                    o = c * TC + s * L
                    last = v.tensor_tensor_scan(hs[:, o:o + L], dec[:, o:o + L], inp[:, o:o + L], 0.0,
                                                ALU.mult, ALU.add)
                last.then_inc(scan_done, 1)

            def weigh(e):
                dve.wait_ge(y_mm, e + 1)
                s = slice(e * ST * D, (e + 1) * ST * D)
                v.tensor_tensor(gathered[:, s].rearrange("p (s d) -> p s d", d=D),
                                yb[:, :].rearrange("p (s d) -> p s d", d=D),
                                p_slot[:, e * ST:(e + 1) * ST].unsqueeze(2).to_broadcast([P, ST, D]),
                                ALU.mult).then_inc(y_done, 1)

            def rows(n):
                dve.wait_ge(rms_std, n + 1)
                if n == 0:
                    dve.wait_ge(gam_in, 16)
                    dve.wait_ge(xn_out, 16 * C)
                v.reciprocal(rms[:, 4 * n:4 * n + 4], rms[:, 4 * n:4 * n + 4]).then_inc(rms_done, 1)
                dve.wait_ge(rms_done, n + 1)
                for i in range(4):
                    t = 4 * n + i
                    v.scalar_tensor_tensor(attn[:, t * D:(t + 1) * D], obank[n % 2][:, i * D:(i + 1) * D],
                                           rms[:, t:t + 1], gam[:, :], ALU.mult, ALU.mult).then_inc(attn_done, 1)

            high_parts()
            conv(3)
            slot_probabilities()
            gated(0)
            gated(1)
            weigh(0)
            clip(0)
            clip(1)
            gated(2)
            gated(3)
            weigh(1)
            clip(2)
            clip(3)
            recur(0)
            weigh(2)
            recur(1)
            rows(0)
            rows(1)
            recur(2)
            weigh(3)
            rows(2)
            rows(3)
            recur(3)
            rows(4)
            weigh(4)
            rows(5)
            rows(6)
            weigh(5)
            rows(7)
            weigh(6)
            weigh(7)


def kernel(**inputs):
    import numpy as _np
    import concourse.bacc as _bacc
    from concourse.bass_utils import run_bass_kernel_spmd as _run

    a = {k[3:]: _np.ascontiguousarray(v) for k, v in inputs.items()}
    params = _np.concatenate([
        a["attn_W_r"].T, a["attn_W_i"].T, a["attn_W_out"].T, a["ffn_Wr"],
        a["attn_conv_w"].reshape(D, TAPS), a["attn_conv_b"].reshape(D, 1), a["attn_b_r"].reshape(D, 1),
        a["attn_b_i"].reshape(D, 1), a["attn_log_a"].reshape(D, 1)], axis=1)
    arrays = {
        "in_x": a["attn_x"],
        "in_params": _np.ascontiguousarray(params),
        "in_gamma": a["attn_gamma"],
        "in_w1": _np.ascontiguousarray(a["ffn_W1"].transpose(1, 0, 2).reshape(P, E * F)),
        "in_w2": _np.ascontiguousarray(a["ffn_W2"].reshape(E, KF, P, D).transpose(2, 0, 1, 3).reshape(P, E * KF * D)),
    }
    nc = _bacc.Bacc("TRN2", target_bir_lowering=False, num_devices=1)
    args = [nc.dram_tensor(n, v.shape, mybir.dt.from_np(v.dtype), kind="ExternalInput").ap()
            for n, v in arrays.items()]
    xn_rows = nc.dram_tensor("xn_rows", (T, D), F32, kind="Internal").ap()
    out = nc.dram_tensor("out_0", (B, L, D), F32, kind="ExternalOutput").ap()
    rglru_moe_kernel(nc, *args, xn_rows, out)
    r = _run(nc, [arrays], core_ids=[0])
    return r.results[0]["out_0"]
```

```python
from contextlib import ExitStack

import concourse.bass as bass
from concourse import mybir

F32 = mybir.dt.float32
I32 = mybir.dt.int32
F16 = mybir.dt.float16
BF16 = mybir.dt.bfloat16
F32R = mybir.dt.float32r
ALU = mybir.AluOpType
ACT = mybir.ActivationFunctionType
AX_X = mybir.AxisListType.X

P = 128
B, L, D = 16, 256, 128
T = B * L
E, F = 8, 512
CAP = T // E
C = 4
J = T // C // P
NT = C * J
TC = T // C
SC = TC // L
HC = TC // 2
KF = F // P
WW = F + KF * D
NW = 4
ST = CAP // P
NS = E * ST
TAPS = 4
Q = P // C
NB = TC // Q
PARTS = 3
PART_STEP = 2.0 ** 11
LN_EPS = 1e-5
RMS_EPS = 1e-6
LOGA_FLOOR = -20.0

WR_T, WI_T, WO_T = 0, D, 2 * D
ROUTER = 3 * D
CONV_W = ROUTER + E
CONV_B, BIAS_R, BIAS_I, LOG_A = (CONV_W + TAPS + i for i in range(4))
NPAR = LOG_A + 1


def rglru_moe_kernel(nc, x, params, gamma, weights, xn_rows, out):
    x_rows = x.rearrange("b l d -> (b l) d")
    out_rows = out.rearrange("b l d -> (b l) d")

    def chunk_rows(dram, c):
        return dram[c * TC:(c + 1) * TC, :].rearrange("(p j) d -> p (j d)", p=P)

    with ExitStack() as ctx:
        def sb(name, shape, dt=F32):
            return ctx.enter_context(nc.sbuf_tensor(name, shape, dt))

        def psum(name):
            return ctx.enter_context(nc.psum_tensor(name, [P, 512], F32))

        def sem(name):
            return ctx.enter_context(nc.semaphore(name))

        par = sb("par", [P, NPAR])
        gam = sb("gam", [P, D])
        w_raw = sb("w_raw", [P, NW, WW])
        w_hi = sb("w_hi", [P, 2, F], F32R)
        w_lo = sb("w_lo", [P, 2, F], F32R)
        x_tok = sb("x_tok", [P, NT * D])
        xn_tok = sb("xn_tok", [P, NT * D])
        xnT = sb("xnT", [P, T])
        xc = sb("xc", [P, T])
        dec = sb("dec", [P, T])
        inp = sb("inp", [P, T])
        sca = sb("sca", [P, T])
        h_sb = sb("h_sb", [P, KF * CAP])
        xg_hi = sb("xg_hi", [P, CAP], F32R)
        xg_lo = sb("xg_lo", [P, CAP], F32R)
        ident = sb("ident", [P, P])
        same_q = sb("same_q", [P, P], BF16)
        below = sb("below", [P, P], BF16)
        earlier_q = sb("earlier_q", [P, P], BF16)
        ones = sb("ones", [P, P], BF16)
        diag = sb("diag", [P, TAPS, P])
        iota_tok = sb("iota_tok", [P, NB])
        chunk_of = sb("chunk_of", [P, 1])
        tok_id = sb("tok_id", [P, NB], F16)
        ecap = sb("ecap", [P, E])
        emask = sb("emask", [P, NB, E])
        bmask = sb("bmask", [P, E, NB])
        eps = sb("eps", [P, 3])
        quarter = eps[:, 2:3]
        stats = sb("stats", [P, NT, 6])
        mv = sb("mv", [P, NT, 2])
        std = sb("std", [P, NT])
        rstd = sb("rstd", [P, NT])
        nmr = sb("nmr", [P, NT])
        half_b = sb("half_b", [P, 2])
        lna = sb("lna", [P, 8])
        top = sb("top", [P, NB])
        eq = sb("eq", [P, NB, E])
        nth = sb("nth", [P, NB, E])
        shifted = sb("shifted", [P, NB, E])
        onehot = sb("onehot", [P, E, NB], BF16)
        in_row = sb("in_row", [P, E])
        in_row16 = sb("in_row16", [P, E], BF16)
        blocks = sb("blocks", [P, E, NB])
        picked = sb("picked", [P, E, NB])
        first = sb("first", [P, NB])
        rank = sb("rank", [P, NB])
        keep = sb("keep", [P, NB])
        slot = sb("slot", [P, NB])
        lost = sb("lost", [P, NB])
        over = sb("over", [P, NB])
        over_lost = sb("over_lost", [P, NB])
        dslot = sb("dslot", [P, NB])
        small = sb("small", [P, 8, E])
        slot_i = sb("slot_i", [P, NB], I32)
        hi_i = sb("hi_i", [P, NB], I32)
        lo_i = sb("lo_i", [P, NB], I32)
        lo16 = sb("lo16", [P, NB], F16)
        hi16 = sb("hi16", [P, NB], F16)
        hi_eq = sb("hi_eq", [P, NS, NB], F16)
        hi_val = sb("hi_val", [P, NS, NB], F16)
        prob = sb("prob", [P, NB])
        part = sb("part", [P, PARTS, NB], F16)
        rest = sb("rest", [P, PARTS, NB])
        idx = sb("idx", [P, NS], I32)
        p_slot = sb("p_slot", [P, NS])
        p_sum = sb("p_sum", [P, NS])
        sq = sb("sq", [P, D])
        ssq = sb("ssq", [P, NT])
        rms = sb("rms", [P, NT])
        lgT = dec[:, TC:2 * TC]
        low_eq = sb("low_eq", [P, P, NB], F16)
        hi_part = xn_tok[:, 0:NB * PARTS * NS // 2].bitcast(F16).rearrange("p (k s b) -> p k s b", k=PARTS, s=NS)
        values = inp[:, 2 * TC:4 * TC].bitcast(F16).rearrange("p (v b) -> p v b", b=NB)
        hs = xnT
        gathered = x_tok
        attn = xn_tok

        tp = [psum("tp0"), psum("tp1")]
        gate = [psum("gate0"), psum("gate1")]
        hid = [psum("hid0"), psum("hid1")]
        two = ctx.enter_context(nc.psum_tensor("two", [P, 2 * HC], F32))
        yb, tb = two[:, 0:HC], two[:, HC:2 * HC]
        in_block = yb[:, 0:E * NB]
        before = tb[:, 0:E * NB]
        totals = tb[:, E * NB:E * NB + E]
        table = yb[:, 0:NS]
        p_table = yb[:, NS:NS + PARTS * NS]
        obank = [gate[0], gate[1], yb]
        hbank = [hid[0], hid[1], tp[1]]

        def tile_of(e, s):
            if e == E - 1 and s >= 1:
                return hbank[s - 1][:, 0:D]
            return tb[:, s * D:(s + 1) * D]

        x_in = [sem(f"x_in{c}") for c in range(C)]
        x_first = sem("x_first")
        par_in = sem("par_in")
        gam_in = sem("gam_in")
        w_in = [sem(f"w_in{e}") for e in range(E)]
        w_hi_done = sem("w_hi_done")
        w_lo_done = sem("w_lo_done")
        xg_lo_done = sem("xg_lo_done")
        x_out = sem("x_out")
        xn_out = sem("xn_out")
        consts = sem("consts")
        fill = sem("fill")
        stat_done = sem("stat_done")
        aggr_done = sem("aggr_done")
        std_done = sem("std_done")
        rstd_done = sem("rstd_done")
        norm_done = sem("norm_done")
        tp_done = sem("tp_done")
        xnT_done = sem("xnT_done")
        logits_done = sem("logits_done")
        psum_clear = sem("psum_clear")
        valued = sem("valued")
        chunked = sem("chunked")
        nmr_done = sem("nmr_done")
        norm_act = sem("norm_act")
        norm_pool = sem("norm_pool")
        diag_done = sem("diag_done")
        conv_mm = sem("conv_mm")
        route = sem("route")
        onehot_done = sem("onehot_done")
        row_done = sem("row_done")
        in_block_done = sem("in_block_done")
        before_done = sem("before_done")
        shift_done = sem("shift_done")
        exp_done = sem("exp_done")
        hi_done = sem("hi_done")
        low_done = sem("low_done")
        table_done = sem("table_done")
        idx_done = sem("idx_done")
        hi_part_done = sem("hi_part_done")
        p_table_done = sem("p_table_done")
        p_slot_done = sem("p_slot_done")
        coef = sem("coef")
        lna_act = sem("lna_act")
        conv_done = sem("conv_done")
        conv_dve = sem("conv_dve")
        conv_pool = sem("conv_pool")
        tap_done = sem("tap_done")
        tap_pool = sem("tap_pool")
        gate_mm = sem("gate_mm")
        gate_free = sem("gate_free")
        decay_done = sem("decay_done")
        square_done = sem("square_done")
        clip_done = sem("clip_done")
        scale_done = sem("scale_done")
        gated_done = sem("gated_done")
        input_done = sem("input_done")
        scan_done = sem("scan_done")
        o_mm = sem("o_mm")
        ssq_done = sem("ssq_done")
        rms_std = sem("rms_std")
        rms_done = sem("rms_done")
        attn_done = sem("attn_done")
        gather_in = [sem(f"gather_in{e}") for e in range(E)]
        xg_tp = sem("xg_tp")
        xg_done = sem("xg_done")
        h_mm = sem("h_mm")
        h_done = sem("h_done")
        y_mm = sem("y_mm")
        y_done = sem("y_done")
        scattered = sem("scattered")
        attn_out = sem("attn_out")

        block = ctx.enter_context(nc.Block())

        DVE_TILES = [(0,)] * (C - 2) + [(0, 1), (0, 1, 4, 5, 6)]
        ACT_TILES = [(1, 4, 5)] * (C - 2) + [(4, 5), (2,)]
        POOL_TILES = [(2, 3, 6, 7)] * (C - 1) + [(3, 7)]

        def normalised(eng, c, half):
            for done, tiles in ((norm_done, DVE_TILES), (norm_act, ACT_TILES), (norm_pool, POOL_TILES)):
                eng.wait_ge(done, sum(len(js) for js in tiles[:c]) + sum(j < 4 * (half + 1) for j in tiles[c]))

        @block.sync
        def _(sp):
            half = J * D // 2
            sp.dma_start(x_tok[:, 0:half], chunk_rows(x_rows, 0)[:, 0:half]).then_inc(x_first, 16)
            sp.dma_start(x_tok[:, half:2 * half], chunk_rows(x_rows, 0)[:, half:]).then_inc(x_in[0], 16)
            for c in range(1, C):
                sp.dma_start(x_tok[:, c * J * D:(c + 1) * J * D], chunk_rows(x_rows, c)).then_inc(x_in[c], 16)
            for c in range(C):
                normalised(sp, c, 1)
                sp.dma_start(chunk_rows(xn_rows, c), xn_tok[:, c * J * D:(c + 1) * J * D]).then_inc(xn_out, 16)
                if c == 0:
                    sp.wait_ge(x_first, 16)
                sp.wait_ge(x_in[c], 16)
                sp.dma_start(chunk_rows(out_rows, c), x_tok[:, c * J * D:(c + 1) * J * D]).then_inc(x_out, 16)
            for e in range(E):
                if e >= NW:
                    sp.wait_ge(y_mm, e - NW + 1)
                sp.dma_start(w_raw[:, e % NW, :], weights[:, e * WW:(e + 1) * WW]).then_inc(w_in[e], 16)

        EPS_CONSTS = 3
        IDENT_CONST = EPS_CONSTS + 1
        EARLY_CONSTS = IDENT_CONST + 4
        CONSTS = EARLY_CONSTS + 3

        POOL_CONV, PE_CONV = 2, 2

        WARM_UP = 28
        GATHERED_AHEAD = 4
        GATE_ORDER = (0, 2, 1, 3)

        def gate_count(c):
            return 4 * GATE_ORDER.index(c)

        def convolved(eng, c, half):
            if c < POOL_CONV:
                eng.wait_ge(conv_pool, (TAPS - 1) * (c + 1))
            elif 2 * c < 2 * POOL_CONV + PE_CONV:
                eng.wait_ge(conv_done, 2 * (c - POOL_CONV) + half + 1)
            else:
                eng.wait_ge(conv_dve, TAPS)

        PE_AT = {3: "project0 project1 project2", 4: "project3", 5: "project7"}
        PE_AFTER = {0: "gates3", 4: "project4 project5 project6"}
        ACT_AT = {0: "decay0 decay1", 1: "decay2 decay3", 2: "scale0", 3: "scale2 scale3 squares0 squares1",
                  4: "squares3", 5: "squares5 squares6 squares7"}
        ACT_AFTER = {0: "gates3", 2: "scale1", 3: "squares2", 4: "squares4"}
        DVE_AT = {1: "clip0 clip1", 2: "gated2", 3: "recur1", 4: "rows1", 5: "rows5 rows6 rows7"}
        DVE_LATE = {0: "gated0", 1: "clip2", 2: "recur0 gated3", 3: "rows0 recur2 recur3", 4: "rows2 rows3"}
        DVE_AFTER = {0: "gated1", 1: "clip3", 4: "rows4"}
        OUTPUT_ORDER = ("expert0 expert1 expert2 expert3 expert4 "
                        "attention0 attention1 attention2 attention3 expert5 expert6 expert7")

        def stages(plan, e, names):
            for word in plan.get(e, "").split():
                stage = word.rstrip("0123456789")
                names[stage](int(word[len(stage):]))

        @block.gpsimd
        def _(pool):
            g = nc.gpsimd
            g.memset(eps[:, 0:1], LN_EPS).then_inc(consts, 1)
            g.memset(eps[:, 1:2], RMS_EPS).then_inc(consts, 1)
            g.memset(eps[:, 2:3], 0.25).then_inc(consts, 1)
            exact = dict(allow_small_or_imprecise_dtypes=True)
            in_q = [[-Q, C], [0, Q]]
            g.memset(ident[:, :], 0.0).then_inc(fill, 1)
            g.memset(ones[:, :], 1.0).then_inc(fill, 1)
            g.memset(emask[:, :, :], 1.0).then_inc(fill, 1)
            g.memset(bmask[:, :, :], 1.0).then_inc(fill, 1)
            pool.wait_ge(fill, 1)
            g.affine_select(out=ident[:, :], in_=ident[:, :], compare_op=ALU.not_equal, fill=1.0, base=0,
                            pattern=[[-1, P]], channel_multiplier=1).then_inc(consts, 1)

            def normalise(c):
                pool.wait_ge(nmr_done, c + 1)
                for j in POOL_TILES[c]:
                    t = c * J + j
                    g.tensor_scalar(xn_tok[:, t * D:(t + 1) * D], x_tok[:, t * D:(t + 1) * D], rstd[:, t:t + 1],
                                    nmr[:, t:t + 1], ALU.mult, ALU.add).then_inc(norm_pool, 1)

            pool.wait_ge(fill, 4)
            g.memset(emask[:, :, 0:1], 0.0).then_inc(consts, 1)
            g.memset(bmask[:, :, 0:1], 0.0).then_inc(consts, 1)
            g.iota(ecap[:, :], [[CAP, E]], base=0, channel_multiplier=0, **exact).then_inc(consts, 1)
            g.iota(iota_tok[:, :], [[Q, NB]], base=-T // 2, channel_multiplier=1, **exact).then_inc(consts, 1)
            early = 3 * P // 4
            g.iota(values[:, 0:early, :], [[1, early], [0, NB]], base=0, channel_multiplier=0,
                   **exact).then_inc(valued, 1)
            normalise(0)
            g.affine_select(out=same_q[:, :], in_=ones[:, :], compare_op=ALU.is_ge, fill=0.0, base=0,
                            pattern=in_q, channel_multiplier=1).then_inc(fill, 1)
            g.affine_select(out=earlier_q[:, :], in_=ones[:, :], compare_op=ALU.is_gt, fill=0.0, base=0,
                            pattern=[[Q, C], [0, Q]], channel_multiplier=-1).then_inc(consts, 1)
            normalise(1)
            pool.wait_ge(fill, 5)
            g.affine_select(out=same_q[:, :], in_=same_q[:, :], compare_op=ALU.is_ge, fill=0.0, base=Q - 1,
                            pattern=[[Q, C], [0, Q]], channel_multiplier=-1).then_inc(consts, 1)
            pool.wait_ge(consts, CONSTS - 1)
            g.tensor_scalar(below[:, :], same_q[:, :], -1.0, 0.0, ALU.mult, ALU.add).then_inc(fill, 1)
            pool.wait_ge(fill, 6)
            g.affine_select(out=below[:, :], in_=below[:, :], compare_op=ALU.is_ge, fill=0.0, base=0,
                            pattern=[[-1, P]], channel_multiplier=1).then_inc(consts, 1)
            normalise(2)
            added = [0]

            def conv(c):
                dst = xc[:, c * TC:(c + 1) * TC].rearrange("d (s l) -> d s l", l=L)
                for back in range(1, TAPS):
                    src = sca[:, back * TC:(back + 1) * TC].rearrange("d (s l) -> d s l", l=L)
                    if c == 0:
                        pool.wait_ge(tap_pool, 1)
                    pool.wait_ge(tap_done, TAPS * c + back)
                    if back > 1:
                        pool.wait_ge(conv_pool, added[0])
                    added[0] += 1
                    g.tensor_tensor(dst[:, :, back:], dst[:, :, back:], src[:, :, 0:L - back],
                                    ALU.add).then_inc(conv_pool, 1)

            normalise(3)
            g.iota(values[:, early:, :], [[1, P - early], [0, NB]], base=early, channel_multiplier=0,
                   **exact).then_inc(valued, 1)
            k = CONV_W + TAPS - 1
            pool.wait_ge(xnT_done, 2)
            pool.wait_ge(par_in, 16)
            g.tensor_scalar(xc[:, 0:TC], xnT[:, 0:TC], par[:, k:k + 1], par[:, CONV_B:CONV_B + 1], ALU.mult,
                            ALU.add).then_inc(tap_pool, 1)
            for c in range(POOL_CONV):
                conv(c)

            def gather(e):
                for s in range(e * ST, (e + 1) * ST):
                    g.indirect_dma_start(gathered[:, s * D:(s + 1) * D], None, xn_rows,
                                         bass.IndirectOffsetOnAxis(ap=idx[:, s:s + 1], axis=0)
                                         ).then_inc(gather_in[e], 16)

            def scatter(e):
                for s in range(e * ST, (e + 1) * ST):
                    pool.wait_ge(y_done, s + 1 if e == E - 1 else ST * (e + 1))
                    g.indirect_dma_start(out_rows, bass.IndirectOffsetOnAxis(ap=idx[:, s:s + 1], axis=0),
                                         gathered[:, s * D:(s + 1) * D], None,
                                         compute_op=ALU.add).then_inc(scattered, 16)

            pool.wait_ge(xn_out, 16 * C)
            pool.wait_ge(x_out, 16 * C)
            pool.wait_ge(idx_done, 1)
            for e in range(GATHERED_AHEAD):
                gather(e)

            def add_expert(e):
                if sent["attention"]:
                    pool.wait_ge(attn_out, 16 * sent["attention"])
                scatter(e)
                sent["experts"] += 1
                if e + GATHERED_AHEAD < E:
                    gather(e + GATHERED_AHEAD)

            def add_attention(c):
                pool.wait_ge(scattered, 16 * ST * sent["experts"])
                pieces = 2 if c == C - 1 else 1
                for piece in range(pieces):
                    tiles = slice(piece * J // pieces * D, (piece + 1) * J // pieces * D)
                    pool.wait_ge(attn_done, J * c + (piece + 1) * J // pieces)
                    g.dma_start(chunk_rows(out_rows, c)[:, tiles], attn[:, c * J * D:(c + 1) * J * D][:, tiles],
                                accum_op=ALU.add).then_inc(attn_out, 16)
                    sent["attention"] += 1

            sent = {"experts": 0, "attention": 0}
            stages({0: OUTPUT_ORDER}, 0, {"expert": add_expert, "attention": add_attention})
            pool.wait_ge(attn_out, 16 * C)
            pool.wait_ge(scattered, 16 * NS)

        @block.tensor
        def _(pe):
            mm = nc.tensor.matmul
            pe.wait_ge(consts, IDENT_CONST)

            def router(n):
                c, half = n // 2, n % 2
                if n == 0:
                    pe.wait_ge(par_in, 16)
                    pe.wait_ge(psum_clear, 1)
                pe.wait_ge(xnT_done, 2 * (c + 1))
                return mm(two[c * Q:c * Q + E, half * HC:(half + 1) * HC], par[:, ROUTER:ROUTER + E],
                          xnT[:, c * TC + half * HC:c * TC + (half + 1) * HC], start=True, stop=True)

            for _ in range(WARM_UP):
                mm(hid[0][:, 0:P], ident[:, :], ident[:, :], start=True, stop=True)
            ROUTER_AFTER = {3: (0, 1), 5: (2, 3), 7: (4, 5)}
            for n in range(2 * C):
                normalised(pe, n // 2, n % 2)
                if n >= 2:
                    pe.wait_ge(xnT_done, n - 1)
                for i in range(4):
                    t = 4 * n + i
                    last = nc.tensor.transpose(tp[n % 2][:, i * P:(i + 1) * P],
                                               xn_tok[:, t * D:(t + 1) * D], ident[:, :])
                last.then_inc(tp_done, 1)
                for m in ROUTER_AFTER.get(n, ()):
                    router(m)
            router(2 * C - 2)
            router(2 * C - 1).then_inc(logits_done, 1)

            def conv(i):
                n = 2 * POOL_CONV + i
                if i == 0:
                    pe.wait_ge(diag_done, TAPS)
                elif i >= 2:
                    pe.wait_ge(conv_done, i - 1)
                cols = slice(n * HC, (n + 1) * HC)
                src = xnT[:, cols].rearrange("d (s l) -> d s l", l=L)
                dst = hid[i % 2][:, :].rearrange("d (s l) -> d s l", l=L)
                mm(hid[i % 2][:, :], diag[:, TAPS - 1, :], xnT[:, cols], start=True, stop=False)
                for back in range(1, TAPS):
                    last = mm(dst[:, :, back:], diag[:, TAPS - 1 - back, :], src[:, :, 0:L - back],
                              start=False, stop=(back == TAPS - 1))
                last.then_inc(conv_mm, 1)

            def gate_half(c, i):
                n = gate_count(c) + i
                convolved(pe, c, i % 2)
                if n >= 2:
                    pe.wait_ge(gate_free, n - 1)
                w = WR_T if i < 2 else WI_T
                mm(gate[n % 2][:, :], par[:, w:w + D], xc[:, c * TC + (i % 2) * HC:c * TC + (i % 2 + 1) * HC],
                   start=True, stop=True).then_inc(gate_mm, 1)

            def gates(c):
                for i in range(4):
                    gate_half(c, i)

            conv(0)
            pe.wait_ge(consts, CONSTS)
            pe.wait_ge(onehot_done, 1)
            oh = onehot[:, :, :].rearrange("p e b -> p (e b)")
            mm(in_block, same_q[:, :], oh, start=True, stop=True).then_inc(in_block_done, 1)
            mm(before, below[:, :], oh, start=True, stop=False)
            pe.wait_ge(row_done, 1)
            mm(before, earlier_q[:, :], in_row16[:, :].unsqueeze(2).to_broadcast([P, E, NB]), start=False, stop=True)
            mm(totals, ones[:, :], in_row16[:, :], start=True, stop=True).then_inc(before_done, 1)
            conv(1)
            gates(0)

            pe.wait_ge(hi_done, 1)
            for b in range(NB):
                pe.wait_ge(low_done, b // (NB // 2) + 1)
                last = mm(table, low_eq[:, :, b], hi_val[:, :, b], start=(b == 0), stop=(b == NB - 1))
            last.then_inc(table_done, 1)

            def p_pass():
                pe.wait_ge(hi_part_done, PARTS)
                for b in range(NB):
                    last = mm(p_table, low_eq[:, :, b], hi_part[:, :, :, b],
                              start=(b == 0), stop=(b == NB - 1))
                last.then_inc(p_table_done, 1)


            def turn(e):
                pe.wait_ge(gather_in[e], 16 * ST)
                if e >= 1:
                    pe.wait_ge(xg_lo_done, e)
                for i in range(ST):
                    s = e * ST + i
                    last = nc.tensor.transpose(tp[0][:, i * P:(i + 1) * P],
                                               gathered[:, s * D:(s + 1) * D], ident[:, :])
                last.then_inc(xg_tp, 1)

            def up(e):
                pe.wait_ge(xg_lo_done, e + 1)
                pe.wait_ge(w_lo_done, e + 1)
                if e == 0:
                    pe.wait_ge(conv_done, PE_CONV)
                for k in range(KF):
                    n = e * KF + k
                    if n >= 3:
                        pe.wait_ge(h_done, n - 2)
                    b = hbank[n % 3][:, :]
                    w = slice(k * P, (k + 1) * P)
                    mm(b, w_hi[:, e % 2, w], xg_hi[:, :], start=True, stop=False)
                    mm(b, w_hi[:, e % 2, w], xg_lo[:, :], start=False, stop=False)
                    mm(b, w_lo[:, e % 2, w], xg_hi[:, :], start=False, stop=True).then_inc(h_mm, 1)

            def down(e):
                if e == 0:
                    pe.wait_ge(hi_done, 1)
                else:
                    pe.wait_ge(y_done, ST * e)
                for s in range(ST):
                    for k in range(KF):
                        if s == 0:
                            pe.wait_ge(h_done, KF * e + k + 1)
                        last = mm(tile_of(e, s), h_sb[:, k * CAP + s * P:k * CAP + (s + 1) * P],
                                  w_raw[:, e % NW, F + k * D:F + (k + 1) * D], start=(k == 0), stop=(k == KF - 1))
                    if s == ST - 1 or e == E - 1:
                        last.then_inc(y_mm, 1)

            def project(n):
                c = n // 2
                pe.wait_ge(scan_done, c + 1)
                if n >= 3:
                    pe.wait_ge(attn_done, 4 * (n - 2))
                else:
                    pe.wait_ge(gate_free, 4 * C)
                    pe.wait_ge(p_slot_done, 1)
                for i in range(4):
                    j = 4 * (n % 2) + i
                    last = mm(obank[n % 3][:, i * D:(i + 1) * D], hs[:, c * TC + j:(c + 1) * TC:J],
                              par[:, WO_T:WO_T + D], start=True, stop=True)
                last.then_inc(o_mm, 1)

            gates(2)
            gates(1)
            turn(0)
            p_pass()
            up(0)
            names = {"gates": gates, "project": project}
            for e in range(E):
                if e + 1 < E:
                    turn(e + 1)
                down(e)
                stages(PE_AT, e, names)
                if e + 1 < E:
                    up(e + 1)
                stages(PE_AFTER, e, names)

        @block.scalar
        def _(act):
            a = nc.scalar.activation
            act.dma_start(par[:, :], params).then_inc(par_in, 16)
            act.dma_start(gam[:, :], gamma.partition_broadcast(P)).then_inc(gam_in, 16)

            def root(c):
                if c == 0:
                    act.wait_ge(consts, EPS_CONSTS)
                act.wait_ge(aggr_done, J * (c + 1))
                a(std[:, c * J:(c + 1) * J], mv[:, c * J:(c + 1) * J, 1], ACT.Sqrt,
                  bias=eps[:, 0:1]).then_inc(std_done, 1)

            def normalise(c):
                act.wait_ge(nmr_done, c + 1)
                for j in ACT_TILES[c]:
                    t = c * J + j
                    a(xn_tok[:, t * D:(t + 1) * D], x_tok[:, t * D:(t + 1) * D], ACT.Identity,
                      scale=rstd[:, t:t + 1], bias=nmr[:, t:t + 1]).then_inc(norm_act, 1)

            def untile(n):
                c = n // 2
                act.wait_ge(tp_done, n + 1)
                dst = xnT[:, c * TC:(c + 1) * TC].rearrange("d (p j) -> d j p", j=J)
                a(dst[:, 4 * (n % 2):4 * (n % 2) + 4, :], tp[n % 2][:, :].rearrange("d (j p) -> d j p", j=4),
                  ACT.Copy).then_inc(xnT_done, 1)

            def tap(c, back):
                src = xnT[:, c * TC:(c + 1) * TC]
                k = CONV_W + TAPS - 1 - back
                if back == 0:
                    act.wait_ge(xnT_done, 2 * (c + 1))
                    ins = a(xc[:, c * TC:(c + 1) * TC], src, ACT.Identity, scale=par[:, k:k + 1],
                            bias=par[:, CONV_B:CONV_B + 1])
                else:
                    if c >= 1:
                        act.wait_ge(conv_pool, (TAPS - 1) * (c - 1) + back)
                    ins = a(sca[:, back * TC:(back + 1) * TC], src, ACT.Identity, scale=par[:, k:k + 1])
                ins.then_inc(tap_done, 1)

            nc.scalar.preload_act_table_set("natural_log_exp_and_others")
            act.wait_ge(coef, 1)
            a(lna[:, 1:2], lna[:, 0:1], ACT.Exp, scale=-1.0).then_inc(lna_act, 1)
            act.wait_ge(coef, 3)
            a(lna[:, 4:5], lna[:, 3:4], ACT.Ln).then_inc(lna_act, 1)
            nc.scalar.preload_act_table_set("sqrt_and_others")

            root(0)
            root(1)
            normalise(0)
            for c in range(1, C - 1):
                root(c + 1)
                normalise(c)
                untile(2 * c - 2)
                untile(2 * c - 1)
            normalise(C - 1)
            untile(2 * C - 4)
            untile(2 * C - 3)
            untile(2 * C - 2)
            untile(2 * C - 1)

            def biased(i):
                act.wait_ge(conv_mm, i + 1)
                n = 2 * POOL_CONV + i
                a(xc[:, n * HC:(n + 1) * HC], hid[i % 2][:, :], ACT.Identity,
                  bias=par[:, CONV_B:CONV_B + 1]).then_inc(conv_done, 1)

            def gates(c):
                if c == 0:
                    act.wait_ge(coef, 7)
                for i, (dst, bias) in enumerate(((dec, 0), (dec, 0), (inp, 1), (inp, 1))):
                    n = gate_count(c) + i
                    act.wait_ge(gate_mm, n + 1)
                    if c == 2 and i == 2:
                        act.wait_ge(low_done, 2)
                    o = c * TC + (i % 2) * HC
                    a(dst[:, o:o + HC], gate[n % 2][:, :], ACT.Tanh, bias=half_b[:, bias:bias + 1],
                      scale=0.5).then_inc(gate_free, 1)

            def decay(c):
                cols = slice(c * TC, (c + 1) * TC)
                act.wait_ge(gate_free, gate_count(c) + 2)
                a(dec[:, cols], dec[:, cols], ACT.Exp, bias=lna[:, 5:6], scale=lna[:, 5:6]).then_inc(decay_done, 1)
                act.wait_ge(decay_done, c + 1)
                act.wait_ge(conv_pool, (TAPS - 1) * POOL_CONV)
                a(sca[:, cols], dec[:, cols], ACT.Square).then_inc(square_done, 1)

            def relu(e):
                for k in range(KF):
                    n = e * KF + k
                    act.wait_ge(h_mm, n + 1)
                    a(h_sb[:, k * CAP:(k + 1) * CAP], hbank[n % 3][:, :], ACT.Relu).then_inc(h_done, 1)

            def lead(e):
                act.wait_ge(w_in[e], 16)
                if e >= 2:
                    act.wait_ge(h_mm, KF * (e - 1))
                a(w_hi[:, e % 2, :], w_raw[:, e % NW, 0:F], ACT.Copy).then_inc(w_hi_done, 1)

            def scale(c):
                cols = slice(c * TC, (c + 1) * TC)
                act.wait_ge(clip_done, c + 1)
                a(sca[:, cols], sca[:, cols], ACT.Sqrt, bias=quarter).then_inc(scale_done, 1)

            def squares(n):
                act.wait_ge(o_mm, n + 1)
                for i in range(4):
                    t = 4 * n + i
                    if t >= 1:
                        act.wait_ge(ssq_done, t)
                    a(sq[:, :], obank[n % 3][:, i * D:(i + 1) * D], ACT.Square,
                      accum_out=ssq[:, t:t + 1]).then_inc(ssq_done, 1)
                act.wait_ge(ssq_done, 4 * (n + 1))
                a(rms[:, 4 * n:4 * n + 4], ssq[:, 4 * n:4 * n + 4], ACT.Sqrt, bias=eps[:, 1:2],
                  scale=1.0 / D).then_inc(rms_std, 1)

            def columns(e):
                act.wait_ge(xg_tp, e + 1)
                a(xg_hi[:, :], tp[0][:, :], ACT.Copy).then_inc(xg_done, 1)

            tap(0, 1)
            tap(0, 2)
            tap(0, 3)
            tap(1, 0)
            tap(1, 1)
            biased(0)
            nc.scalar.preload_act_table_set("exp_and_others")
            act.wait_ge(shift_done, 1)
            a(shifted[:, :, :], shifted[:, :, :], ACT.Exp).then_inc(exp_done, 1)
            tap(1, 2)
            tap(1, 3)
            biased(1)
            gates(0)
            gates(2)
            lead(0)
            gates(1)
            columns(0)
            lead(1)
            relu(0)
            names = {"gates": gates, "decay": decay, "scale": scale, "squares": squares}
            for e in range(E):
                if e + 1 < E:
                    columns(e + 1)
                stages(ACT_AT, e, names)
                if e + 1 < E:
                    relu(e + 1)
                if e + 2 < E:
                    lead(e + 2)
                stages(ACT_AFTER, e, names)

        @block.vector
        def _(dve):
            v = nc.vector

            for q in range(C):
                v.memset(chunk_of[q * Q:(q + 1) * Q, :], float((TC - Q) * q)).then_inc(chunked, 1)
            v.memset(two[:, :], 0.0).then_inc(psum_clear, 1)
            log_a = par[:, LOG_A:LOG_A + 1]

            def hold():
                dve.wait_ge(par_in, 16)
                v.tensor_scalar(lna[:, 0:1], log_a, LOGA_FLOOR, None, ALU.max).then_inc(coef, 1)

            def add_one():
                dve.wait_ge(lna_act, 1)
                v.tensor_scalar(lna[:, 2:3], lna[:, 1:2], 1.0, None, ALU.add).then_inc(coef, 1)

            def invert():
                dve.wait_ge(coef, 2)
                v.reciprocal(lna[:, 3:4], lna[:, 2:3]).then_inc(coef, 1)

            coefficient = {3: hold, 5: add_one, 6: invert}

            def moments(c):
                for t in range(c * J, (c + 1) * J):
                    if t == 0:
                        dve.wait_ge(x_first, 16)
                    elif t == J // 2 or t % J == 0:
                        dve.wait_ge(x_in[c], 16)
                    v.bn_stats(stats[:, t, :], x_tok[:, t * D:(t + 1) * D]).then_inc(stat_done, 1)
                    if t in coefficient:
                        coefficient[t]()
                for t in range(c * J, (c + 1) * J):
                    dve.wait_ge(stat_done, t + 1)
                    v.bn_aggr(mv[:, t, :], stats[:, t, :]).then_inc(aggr_done, 1)

            def normalise(c):
                dve.wait_ge(std_done, c + 1)
                v.reciprocal(rstd[:, c * J:(c + 1) * J], std[:, c * J:(c + 1) * J]).then_inc(rstd_done, 1)
                dve.wait_ge(rstd_done, c + 1)
                cols = slice(c * J, (c + 1) * J)
                v.scalar_tensor_tensor(nmr[:, cols], mv[:, cols, 0], -1.0, rstd[:, cols], ALU.mult,
                                       ALU.mult).then_inc(nmr_done, 1)
                for j in DVE_TILES[c]:
                    t = c * J + j
                    v.tensor_scalar(xn_tok[:, t * D:(t + 1) * D], x_tok[:, t * D:(t + 1) * D], mv[:, t, 0:1],
                                    rstd[:, t:t + 1], ALU.subtract, ALU.mult).then_inc(norm_done, 1)

            moments(0)
            moments(1)
            normalise(0)
            moments(2)
            normalise(1)
            moments(3)
            normalise(2)
            normalise(3)

            dve.wait_ge(consts, IDENT_CONST)
            for k in range(TAPS):
                v.tensor_scalar(diag[:, k, :], ident[:, :], par[:, CONV_W + k:CONV_W + k + 1], None,
                                ALU.mult).then_inc(diag_done, 1)
            v.tensor_scalar(lna[:, 6:7], log_a, -LOGA_FLOOR, 0.0, ALU.add, ALU.min).then_inc(coef, 1)
            v.tensor_scalar(half_b[:, :], par[:, BIAS_R:BIAS_I + 1], 0.5, None, ALU.mult).then_inc(coef, 1)
            dve.wait_ge(coef, 5)
            dve.wait_ge(lna_act, 2)
            v.tensor_scalar(lna[:, 5:6], lna[:, 4:5], lna[:, 6:7], 4.0, ALU.add, ALU.mult).then_inc(coef, 1)
            dve.wait_ge(consts, EARLY_CONSTS)
            dve.wait_ge(chunked, C)
            v.tensor_scalar(tok_id[:, :], iota_tok[:, :], chunk_of[:, 0:1], None, ALU.add).then_inc(coef, 1)
            dve.wait_ge(coef, 7)

            results = [0]

            def put(ins):
                results[0] += 1
                ins.then_inc(route, 1)
                return results[0]

            def need(n):
                dve.wait_ge(route, n)

            def per_token(ap):
                return ap.unsqueeze(2).to_broadcast([P, NB, E])

            def per_token_eb(ap):
                return ap.unsqueeze(1).to_broadcast([P, E, NB])

            def per_expert(ap):
                return ap.unsqueeze(2).to_broadcast([P, E, NB])

            def over_experts(ap):
                return ap.rearrange("p e b -> p b e")

            dve.wait_ge(logits_done, 1)
            need(put(v.transpose(lgT, two[:, :])))
            lg = lgT.rearrange("p (b w) -> p b w", w=Q)[:, :, 0:E]
            need(put(v.tensor_reduce(top[:, :], lg, AX_X, ALU.max)))
            equal = put(v.tensor_tensor(eq[:, :, :], lg, per_token(top[:, :]), ALU.is_equal))
            v.tensor_tensor(shifted[:, :, :], lg, per_token(top[:, :]), ALU.subtract).then_inc(shift_done, 1)
            need(equal)
            need(put(v.tensor_tensor_scan(nth[:, :, :].rearrange("p b e -> p (b e)"),
                                          emask[:, :, :].rearrange("p b e -> p (b e)"),
                                          eq[:, :, :].rearrange("p b e -> p (b e)"), 0.0, ALU.mult, ALU.add)))
            v.scalar_tensor_tensor(over_experts(onehot[:, :, :]), nth[:, :, :], 1.0, eq[:, :, :], ALU.is_equal,
                                   ALU.mult).then_inc(onehot_done, 1)
            dve.wait_ge(onehot_done, 1)
            need(put(v.tensor_reduce(in_row[:, :], onehot[:, :, :], AX_X, ALU.add)))
            v.tensor_copy(in_row16[:, :], in_row[:, :]).then_inc(row_done, 1)
            product = put(v.tensor_tensor(picked[:, :, :], onehot[:, :, :], per_expert(ecap[:, :]), ALU.mult))
            dve.wait_ge(in_block_done, 1)
            counted = put(v.tensor_tensor_scan(blocks[:, :, :].rearrange("p e b -> p (e b)"),
                                               bmask[:, :, :].rearrange("p e b -> p (e b)"),
                                               in_block, 0.0, ALU.mult, ALU.add))
            need(product)
            based = put(v.tensor_reduce(first[:, :], over_experts(picked[:, :, :]), AX_X, ALU.add))
            kept, free, drop, free_before, drop_before, one = (small[:, i, :] for i in range(6))
            unit = put(v.memset(small[:, 5:6, :], 1.0))
            dve.wait_ge(before_done, 1)
            kept_n = put(v.tensor_scalar(kept, totals, float(CAP), None, ALU.min))
            need(counted)
            wide = put(v.tensor_tensor(blocks[:, :, :].rearrange("p e b -> p (e b)"),
                                       blocks[:, :, :].rearrange("p e b -> p (e b)"), before, ALU.add))
            need(kept_n)
            free_n = put(v.tensor_scalar(free, kept, -1.0, float(CAP), ALU.mult, ALU.add))
            drop_n = put(v.tensor_tensor(drop, totals, kept, ALU.subtract))
            need(wide)
            product = put(v.tensor_tensor(picked[:, :, :], blocks[:, :, :], onehot[:, :, :], ALU.mult))
            need(max(free_n, drop_n, unit))
            fsum = put(v.tensor_tensor_scan(free_before, one, free, 0.0, ALU.mult, ALU.add))
            dsum = put(v.tensor_tensor_scan(drop_before, one, drop, 0.0, ALU.mult, ALU.add))
            need(product)
            ranked = put(v.tensor_reduce(rank[:, :], over_experts(picked[:, :, :]), AX_X, ALU.add))
            need(fsum)
            fbefore = put(v.tensor_tensor(free_before, free_before, free, ALU.subtract))
            need(dsum)
            need(put(v.tensor_tensor(drop_before, drop_before, drop, ALU.subtract)))
            need(ranked)
            product = put(v.tensor_tensor(picked[:, :, :], per_expert(drop_before), onehot[:, :, :], ALU.mult))
            kept_tok = put(v.tensor_scalar(keep[:, :], rank[:, :], float(CAP), None, ALU.is_lt))
            need(based)
            slotted = put(v.tensor_tensor(slot[:, :], rank[:, :], first[:, :], ALU.add))
            need(product)
            over_n = put(v.tensor_reduce(over[:, :], over_experts(picked[:, :, :]), AX_X, ALU.add))
            need(max(kept_tok, slotted))
            lost_n = put(v.tensor_scalar(lost[:, :], keep[:, :], -1.0, 1.0, ALU.mult, ALU.add))
            need(over_n)
            over_n = put(v.scalar_tensor_tensor(over[:, :], rank[:, :], -float(CAP), over[:, :], ALU.add, ALU.add))
            slotted = put(v.tensor_tensor(slot[:, :], slot[:, :], keep[:, :], ALU.mult))
            need(max(fbefore, over_n))
            place = put(v.tensor_tensor(picked[:, :, :], per_token_eb(over[:, :]), per_expert(free_before), ALU.is_ge))
            need(lost_n)
            lost_over = put(v.tensor_tensor(over_lost[:, :], over[:, :], lost[:, :], ALU.mult))
            need(place)
            place = put(v.tensor_tensor(picked[:, :, :], picked[:, :, :], per_expert(kept), ALU.mult))
            need(max(lost_over, slotted))
            slotted = put(v.tensor_tensor(slot[:, :], slot[:, :], over_lost[:, :], ALU.add))
            need(place)
            need(put(v.tensor_reduce(dslot[:, :], over_experts(picked[:, :, :]), AX_X, ALU.add)))
            need(put(v.tensor_tensor(dslot[:, :], dslot[:, :], lost[:, :], ALU.mult)))
            need(slotted)
            need(put(v.tensor_tensor(slot_i[:, :], slot[:, :], dslot[:, :], ALU.add)))
            low = put(v.tensor_scalar(lo_i[:, :], slot_i[:, :], P - 1, None, ALU.bitwise_and))
            high = put(v.tensor_scalar(hi_i[:, :], slot_i[:, :], 7, None, ALU.logical_shift_right))
            need(low)
            low = put(v.tensor_copy(lo16[:, :], lo_i[:, :]))
            need(high)
            high = put(v.tensor_copy(hi16[:, :], hi_i[:, :]))

            def per_value(ap, n):
                return ap.unsqueeze(1).to_broadcast([P, n, ap.shape[-1]])

            dve.wait_ge(valued, 2)
            need(high)
            need(put(v.tensor_tensor(hi_eq[:, :, :], values[:, 0:NS, :], per_value(hi16[:, :], NS), ALU.is_equal)))
            v.tensor_tensor(hi_val[:, :, :], hi_eq[:, :, :], per_value(tok_id[:, :], NS), ALU.mult).then_inc(hi_done, 1)
            need(low)
            for half in range(2):
                b = slice(half * NB // 2, (half + 1) * NB // 2)
                v.tensor_tensor(low_eq[:, :, b], values[:, :, b], per_value(lo16[:, b], P),
                                ALU.is_equal).then_inc(low_done, 1)

            dve.wait_ge(table_done, 1)
            v.tensor_scalar(idx[:, :], table, float(T // 2), None, ALU.add).then_inc(idx_done, 1)
            dve.wait_ge(exp_done, 1)
            need(put(v.tensor_reduce(top[:, :], shifted[:, :, :], AX_X, ALU.add)))
            need(put(v.reciprocal(prob[:, :], top[:, :])))
            need(put(v.tensor_tensor(rest[:, 0, :], prob[:, :], keep[:, :], ALU.mult)))
            for k in range(PARTS):
                need(put(v.tensor_copy(part[:, k, :], rest[:, k, :])))
                if k + 1 < PARTS:
                    need(put(v.tensor_tensor(rest[:, k + 1, :], rest[:, k, :], part[:, k, :], ALU.subtract)))
                    need(put(v.tensor_scalar(rest[:, k + 1, :], rest[:, k + 1, :], PART_STEP, None, ALU.mult)))

            def tap(back):
                cols = slice((C - 1) * TC, T)
                src = xnT[:, cols].rearrange("d (s l) -> d s l", l=L)
                dst = xc[:, cols].rearrange("d (s l) -> d s l", l=L)
                k = CONV_W + TAPS - 1 - back
                if back == 0:
                    v.tensor_scalar(xc[:, cols], xnT[:, cols], par[:, k:k + 1], par[:, CONV_B:CONV_B + 1],
                                    ALU.mult, ALU.add).then_inc(conv_dve, 1)
                else:
                    dve.wait_ge(conv_dve, back)
                    v.scalar_tensor_tensor(dst[:, :, back:], src[:, :, 0:L - back], par[:, k:k + 1], dst[:, :, back:],
                                           ALU.mult, ALU.add).then_inc(conv_dve, 1)

            def high_parts():
                dve.wait_ge(xn_out, 16 * C)
                for k in range(PARTS):
                    v.tensor_tensor(hi_part[:, k, :, :], hi_eq[:, :, :], per_value(part[:, k, :], NS),
                                    ALU.mult).then_inc(hi_part_done, 1)

            def slot_probabilities():
                dve.wait_ge(p_table_done, 1)
                pt = p_table.rearrange("p (k s) -> p k s", s=NS)
                need(put(v.tensor_copy(p_sum[:, :], pt[:, PARTS - 1, :])))
                for k in range(PARTS - 2, -1, -1):
                    ins = v.scalar_tensor_tensor(p_sum[:, :] if k else p_slot[:, :], p_sum[:, :], 1.0 / PART_STEP,
                                                 pt[:, k, :], ALU.mult, ALU.add)
                    if k:
                        need(put(ins))
                    else:
                        ins.then_inc(p_slot_done, 1)
                dve.wait_ge(p_slot_done, 1)

            def weights_rest(e):
                dve.wait_ge(w_hi_done, e + 1)
                v.tensor_tensor(w_lo[:, e % 2, :], w_raw[:, e % NW, 0:F], w_hi[:, e % 2, :].bitcast(F32),
                                ALU.subtract).then_inc(w_lo_done, 1)

            def columns_rest(e):
                dve.wait_ge(xg_done, e + 1)
                v.tensor_tensor(xg_lo[:, :], tp[0][:, :], xg_hi[:, :].bitcast(F32),
                                ALU.subtract).then_inc(xg_lo_done, 1)

            def clip(c):
                cols = slice(c * TC, (c + 1) * TC)
                dve.wait_ge(square_done, c + 1)
                v.tensor_scalar(sca[:, cols], sca[:, cols], 1.0, -0.25, ALU.min, ALU.mult).then_inc(clip_done, 1)

            def gated(c):
                cols = slice(c * TC, (c + 1) * TC)
                dve.wait_ge(gate_free, gate_count(c) + 4)
                if 2 * c < 2 * POOL_CONV + PE_CONV:
                    convolved(dve, c, 1)
                v.scalar_tensor_tensor(inp[:, cols], inp[:, cols], 1.0, xc[:, cols], ALU.add,
                                       ALU.mult).then_inc(gated_done, 1)

            def recur(c):
                cols = slice(c * TC, (c + 1) * TC)
                dve.wait_ge(scale_done, c + 1)
                dve.wait_ge(gated_done, c + 1)
                v.tensor_tensor(inp[:, cols], inp[:, cols], sca[:, cols], ALU.mult).then_inc(input_done, 1)
                dve.wait_ge(input_done, c + 1)
                for s in range(SC):
                    o = c * TC + s * L
                    last = v.tensor_tensor_scan(hs[:, o:o + L], dec[:, o:o + L], inp[:, o:o + L], 0.0,
                                                ALU.mult, ALU.add)
                last.then_inc(scan_done, 1)

            def weigh(e):
                if e < E - 1:
                    dve.wait_ge(y_mm, e + 1)
                    s = slice(e * ST * D, (e + 1) * ST * D)
                    v.tensor_tensor(gathered[:, s].rearrange("p (s d) -> p s d", d=D),
                                    tb[:, :].rearrange("p (s d) -> p s d", d=D),
                                    p_slot[:, e * ST:(e + 1) * ST].unsqueeze(2).to_broadcast([P, ST, D]),
                                    ALU.mult).then_inc(y_done, ST)
                    return
                for s in range(ST):
                    dve.wait_ge(y_mm, e + 1 + s)
                    t = e * ST + s
                    v.tensor_scalar(gathered[:, t * D:(t + 1) * D], tile_of(e, s), p_slot[:, t:t + 1], None,
                                    ALU.mult).then_inc(y_done, 1)

            def rows(n):
                dve.wait_ge(rms_std, n + 1)
                if n == 0:
                    dve.wait_ge(gam_in, 16)
                    dve.wait_ge(xn_out, 16 * C)
                v.reciprocal(rms[:, 4 * n:4 * n + 4], rms[:, 4 * n:4 * n + 4]).then_inc(rms_done, 1)
                dve.wait_ge(rms_done, n + 1)
                for i in range(4):
                    t = 4 * n + i
                    v.scalar_tensor_tensor(attn[:, t * D:(t + 1) * D], obank[n % 3][:, i * D:(i + 1) * D],
                                           rms[:, t:t + 1], gam[:, :], ALU.mult, ALU.mult).then_inc(attn_done, 1)

            high_parts()
            weights_rest(0)
            tap(0)
            tap(1)
            columns_rest(0)
            weights_rest(1)
            slot_probabilities()
            tap(2)
            tap(3)
            names = {"gated": gated, "clip": clip, "recur": recur, "rows": rows}
            for e in range(E):
                if e + 1 < E:
                    columns_rest(e + 1)
                stages(DVE_AT, e, names)
                weigh(e)
                stages(DVE_LATE, e, names)
                if e + 2 < E:
                    weights_rest(e + 2)
                stages(DVE_AFTER, e, names)


def kernel(**inputs):
    import numpy as _np
    import concourse.bacc as _bacc
    from concourse.bass_utils import run_bass_kernel_spmd as _run

    a = {k[3:]: _np.ascontiguousarray(v) for k, v in inputs.items()}
    params = _np.concatenate([
        a["attn_W_r"].T, a["attn_W_i"].T, a["attn_W_out"].T, a["ffn_Wr"],
        a["attn_conv_w"].reshape(D, TAPS), a["attn_conv_b"].reshape(D, 1), a["attn_b_r"].reshape(D, 1),
        a["attn_b_i"].reshape(D, 1), a["attn_log_a"].reshape(D, 1)], axis=1)
    arrays = {
        "in_x": a["attn_x"],
        "in_params": _np.ascontiguousarray(params),
        "in_gamma": a["attn_gamma"],
        "in_weights": _np.ascontiguousarray(_np.concatenate([
            a["ffn_W1"].transpose(1, 0, 2),
            a["ffn_W2"].reshape(E, KF, P, D).transpose(2, 0, 1, 3).reshape(P, E, KF * D)], axis=2).reshape(P, E * WW)),
    }
    nc = _bacc.Bacc("TRN2", target_bir_lowering=False, num_devices=1)
    args = [nc.dram_tensor(n, v.shape, mybir.dt.from_np(v.dtype), kind="ExternalInput").ap()
            for n, v in arrays.items()]
    xn_rows = nc.dram_tensor("xn_rows", (T, D), F32, kind="Internal").ap()
    out = nc.dram_tensor("out_0", (B, L, D), F32, kind="ExternalOutput").ap()
    rglru_moe_kernel(nc, *args, xn_rows, out)
    r = _run(nc, [arrays], core_ids=[0])
    return r.results[0]["out_0"]
```
